# Optimizing a Trainium2 kernel written in Bass

```python
import numpy as np
import jax
import jax.numpy as jnp

def _softmax(x, axis=-1):
    return jax.nn.softmax(x, axis=axis)

def _gelu(x):
    return jax.nn.gelu(x, approximate=True)

def _silu(x):
    return jax.nn.silu(x)

def _sigmoid(x):
    return jax.nn.sigmoid(x)

def _layernorm(x, axis=-1, eps=1e-05):
    m = jnp.mean(x, axis=axis, keepdims=True)
    v = jnp.var(x, axis=axis, keepdims=True)
    return (x - m) / jnp.sqrt(v + eps)

def _scatter_add(tgt, idx, src, axis=0):
    return tgt.at[idx].add(src)

def _segment_sum(src, seg, n):
    return jax.ops.segment_sum(src, seg, n)
kernel_name = 'mk_cond_resid_d2_seqx_r2_2a1741'

def setup_inputs(seed: int=0):
    np.random.seed(seed)
    _w = jnp.asarray

    def _rec_inputs():
        import jax
        import jax.numpy as jnp
        _rk = jax.random.key(seed)
        x = -0.000125 + 0.9999 * jax.random.normal(jax.random.fold_in(_rk, 1), (2, 2048, 512), jnp.float32)
        _lenS = 2048 - jax.random.randint(jax.random.fold_in(_rk, 7), (2,), 0, max(1, 2048 // 4) + 1, jnp.int32)
        _lenS2 = 2048 - jax.random.randint(jax.random.fold_in(_rk, 8), (2,), 0, max(1, 2048 // 4) + 1, jnp.int32)
        cond_1024 = -0.00493535 + 1.00056 * jax.random.normal(jax.random.fold_in(_rk, 11), (2, 512), jnp.float32)
        return (x, cond_1024)
    x, cond_1024 = _rec_inputs()

    def _L0_cond_setup():
        import jax, jax.numpy as jnp
        import numpy as np
        N, T, D, H = (64, 256, 512, 512)

        def lstm_scan(x, h0, Wx, Wh, b):
            xW = jnp.einsum('ntd,dg->ntg', x, Wx) + b
            Hdim = h0.shape[1]
            c0 = jnp.zeros_like(h0)

            def step(carry, xw_t):
                prev_h, prev_c = carry
                a = xw_t + prev_h @ Wh
                i = jax.nn.sigmoid(a[:, :Hdim])
                f = jax.nn.sigmoid(a[:, Hdim:2 * Hdim])
                o = jax.nn.sigmoid(a[:, 2 * Hdim:3 * Hdim])
                g = jnp.tanh(a[:, 3 * Hdim:])
                next_c = f * prev_c + i * g
                next_h = o * jnp.tanh(next_c)
                return ((next_h, next_c), next_h)
            _, hs = jax.lax.scan(step, (h0, c0), jnp.swapaxes(xW, 0, 1))
            return jnp.swapaxes(hs, 0, 1)
        key = jax.random.key(seed)
        k1, k2, k3, k4 = jax.random.split(key, 4)
        x = jax.random.normal(k1, (N, T, D), dtype=jnp.float32)
        h0 = jax.random.normal(k2, (N, H), dtype=jnp.float32)
        Wx = jax.random.normal(k3, (D, 4 * H), dtype=jnp.float32) / np.sqrt(D)
        Wh = jax.random.normal(k4, (H, 4 * H), dtype=jnp.float32) / np.sqrt(H)
        b = jnp.zeros((4 * H,), dtype=jnp.float32)
        return {'x': x, 'h0': h0, 'Wx': Wx, 'Wh': Wh, 'b': b}
    _L0_cond_all = _L0_cond_setup()
    _L0_cond_in = {k: v for k, v in _L0_cond_all.items() if k in ('Wx', 'Wh', 'b')}
    del _L0_cond_all

    def _L1_cond_setup():
        import jax, jax.numpy as jnp
        import numpy as np
        INPUT_DIM = 512
        HIDDEN_DIM = 512
        CHUNK_SIZE = 4

        def _linear_params(key, fan_in, fan_out):
            kw, kb = jax.random.split(key)
            bound = 1.0 / np.sqrt(fan_in)
            W = jax.random.uniform(kw, (fan_in, fan_out), jnp.float32, -bound, bound)
            b = jax.random.uniform(kb, (fan_out,), jnp.float32, -bound, bound)
            return (W, b)

        def _gru_forward(x, h0, Wz, bz, Wr, br, Wh, bh, Wp, bp):
            B, T, D = x.shape
            t = jnp.arange(T)
            do_prop = ((t + 1) % CHUNK_SIZE == 0) & (t < T - 1)
            xs = jnp.transpose(x, (1, 0, 2))

            def step(h, inp):
                x_t, prop = inp
                comb = jnp.concatenate([x_t, h], axis=-1)
                z = jax.nn.sigmoid(comb @ Wz + bz)
                r = jax.nn.sigmoid(comb @ Wr + br)
                comb2 = jnp.concatenate([x_t, r * h], axis=-1)
                h_cand = jnp.tanh(comb2 @ Wh + bh)
                h_new = (1.0 - z) * h + z * h_cand
                h_next = jnp.where(prop, jnp.tanh(h_new @ Wp + bp), h_new)
                return (h_next, h_new)
            _, ys = jax.lax.scan(step, h0, (xs, do_prop))
            return jnp.transpose(ys, (1, 0, 2))
        key = jax.random.key(seed)
        ks = jax.random.split(key, 6)
        x = jax.random.normal(ks[0], (64, 256, INPUT_DIM), jnp.float32)
        h0 = jax.random.normal(ks[1], (64, HIDDEN_DIM), jnp.float32)
        Wz, bz = _linear_params(ks[2], INPUT_DIM + HIDDEN_DIM, HIDDEN_DIM)
        Wr, br = _linear_params(ks[3], INPUT_DIM + HIDDEN_DIM, HIDDEN_DIM)
        Wh, bh = _linear_params(ks[4], INPUT_DIM + HIDDEN_DIM, HIDDEN_DIM)
        Wp, bp = _linear_params(ks[5], HIDDEN_DIM, HIDDEN_DIM)
        return {'x': x, 'h0': h0, 'Wz': Wz, 'bz': bz, 'Wr': Wr, 'br': br, 'Wh': Wh, 'bh': bh, 'Wp': Wp, 'bp': bp}
    _L1_cond_all = _L1_cond_setup()
    _L1_cond_in = {k: v for k, v in _L1_cond_all.items() if k in ('Wz', 'bz', 'Wr', 'br', 'Wh', 'bh', 'Wp', 'bp')}
    del _L1_cond_all
    return {'x': x, 'cond_1024': cond_1024, 'L0_cond_Wx': _L0_cond_in['Wx'], 'L0_cond_Wh': _L0_cond_in['Wh'], 'L0_cond_b': _L0_cond_in['b'], 'L1_cond_Wz': _L1_cond_in['Wz'], 'L1_cond_bz': _L1_cond_in['bz'], 'L1_cond_Wr': _L1_cond_in['Wr'], 'L1_cond_br': _L1_cond_in['br'], 'L1_cond_Wh': _L1_cond_in['Wh'], 'L1_cond_bh': _L1_cond_in['bh'], 'L1_cond_Wp': _L1_cond_in['Wp'], 'L1_cond_bp': _L1_cond_in['bp']}

def reference(x, cond_1024, L0_cond_Wx, L0_cond_Wh, L0_cond_b, L1_cond_Wz, L1_cond_bz, L1_cond_Wr, L1_cond_br, L1_cond_Wh, L1_cond_bh, L1_cond_Wp, L1_cond_bp):
    import jax
    import jax.numpy as jnp

    def _L0_cond_ref(x, h0, Wx, Wh, b):
        import jax, jax.numpy as jnp
        import numpy as np
        N, T, D, H = (64, 256, 512, 512)

        def lstm_scan(x, h0, Wx, Wh, b):
            xW = jnp.einsum('ntd,dg->ntg', x, Wx) + b
            Hdim = h0.shape[1]
            c0 = jnp.zeros_like(h0)

            def step(carry, xw_t):
                prev_h, prev_c = carry
                a = xw_t + prev_h @ Wh
                i = jax.nn.sigmoid(a[:, :Hdim])
                f = jax.nn.sigmoid(a[:, Hdim:2 * Hdim])
                o = jax.nn.sigmoid(a[:, 2 * Hdim:3 * Hdim])
                g = jnp.tanh(a[:, 3 * Hdim:])
                next_c = f * prev_c + i * g
                next_h = o * jnp.tanh(next_c)
                return ((next_h, next_c), next_h)
            _, hs = jax.lax.scan(step, (h0, c0), jnp.swapaxes(xW, 0, 1))
            return jnp.swapaxes(hs, 0, 1)
        return lstm_scan(x, h0, Wx, Wh, b)

    def _L1_cond_ref(x, h0, Wz, bz, Wr, br, Wh, bh, Wp, bp):
        import jax, jax.numpy as jnp
        import numpy as np
        INPUT_DIM = 512
        HIDDEN_DIM = 512
        CHUNK_SIZE = 4

        def _linear_params(key, fan_in, fan_out):
            kw, kb = jax.random.split(key)
            bound = 1.0 / np.sqrt(fan_in)
            W = jax.random.uniform(kw, (fan_in, fan_out), jnp.float32, -bound, bound)
            b = jax.random.uniform(kb, (fan_out,), jnp.float32, -bound, bound)
            return (W, b)

        def _gru_forward(x, h0, Wz, bz, Wr, br, Wh, bh, Wp, bp):
            B, T, D = x.shape
            t = jnp.arange(T)
            do_prop = ((t + 1) % CHUNK_SIZE == 0) & (t < T - 1)
            xs = jnp.transpose(x, (1, 0, 2))

            def step(h, inp):
                x_t, prop = inp
                comb = jnp.concatenate([x_t, h], axis=-1)
                z = jax.nn.sigmoid(comb @ Wz + bz)
                r = jax.nn.sigmoid(comb @ Wr + br)
                comb2 = jnp.concatenate([x_t, r * h], axis=-1)
                h_cand = jnp.tanh(comb2 @ Wh + bh)
                h_new = (1.0 - z) * h + z * h_cand
                h_next = jnp.where(prop, jnp.tanh(h_new @ Wp + bp), h_new)
                return (h_next, h_new)
            _, ys = jax.lax.scan(step, h0, (xs, do_prop))
            return jnp.transpose(ys, (1, 0, 2))
        return _gru_forward(x, h0, Wz, bz, Wr, br, Wh, bh, Wp, bp)
    x = x + _L0_cond_ref(x, cond_1024, L0_cond_Wx, L0_cond_Wh, L0_cond_b)
    x = x + _L1_cond_ref(x, cond_1024, L1_cond_Wz, L1_cond_bz, L1_cond_Wr, L1_cond_br, L1_cond_Wh, L1_cond_bh, L1_cond_Wp, L1_cond_bp)
    return x

_drawn_inputs = setup_inputs


def setup_inputs(seed=0):
    import zlib

    import numpy as np

    out = dict(_drawn_inputs(seed))
    spreads = {'L0_cond_b': (0.0, 0.1)}
    factors = {'cond_1024': 4.068,
     'L1_cond_bz': 28.912,
     'L1_cond_Wr': 23.344,
     'L1_cond_br': 64.0,
     'L1_cond_bh': 4.489,
     'L1_cond_bp': 7.746}
    for name, (base, spread) in spreads.items():
        noise = np.random.default_rng([zlib.crc32(name.encode()), seed]).standard_normal(out[name].shape)
        drawn = base * np.exp(spread * noise) if base else spread * noise
        out[name] = jnp.asarray(drawn.astype(out[name].dtype))
    for name, factor in factors.items():
        out[name] = (out[name] * factor).astype(out[name].dtype)
    return out
```

```python
from contextlib import ExitStack

import concourse.bass as bass
from concourse import mybir

P = 128
F32 = mybir.dt.float32
F16 = mybir.dt.float16
I32 = mybir.dt.int32
ACT = mybir.ActivationFunctionType
ALU = mybir.AluOpType
AX = mybir.AxisListType
RMAX = bass.bass_isa.ReduceOp.max

B = 2
D = 512
N = D // P
NB = N * B
LG = 4
GG = 3
BT = 16
BC = BT * NB
PIECE = N * D
XRING = 4
LAG = 2

EXPONENT = 0x7F800000
TINY = 2.0 ** -40
LSTM_H = 2.0 ** 15
GRU_H = 2.0 ** 14

K_WHL, K_WHG, K_WXL, K_WXG, K_X, K_H0 = 0, 1, 5, 9, 12, 13
NK = 14


def cond_resid_kernel(nc, x, h0, w_lstm_x, w_lstm_h, b_lstm, w_gru_x, w_gru_h, b_gru, b_prop, out):
    T = x.shape[1] // NB
    NBLK = T // BT
    with ExitStack() as ctx:
        def sb(name, shape, dt=F32):
            return ctx.enter_context(nc.sbuf_tensor(name, shape, dt))

        def psum(name, shape):
            return ctx.enter_context(nc.psum_tensor(name, shape, F32))

        def sem(name):
            return ctx.enter_context(nc.semaphore(name))

        whl = [sb(f"whl{w}", [P, LG, N, D], F16) for w in range(2)]
        whg = [sb(f"whg{w}", [P, GG + 1, N, D], F16) for w in range(2)]
        wxl = [sb(f"wxl{w}", [P, LG, N, N, P], F16) for w in range(2)]
        wxg = [sb(f"wxg{w}", [P, GG, N, N, P], F16) for w in range(2)]
        NST = 4
        stage = sb("stage", [P, NST, PIECE])

        piece_max = sb("piece_max", [P, 24])
        core_max = sb("core_max", [P, 24])
        largest = sb("largest", [P, NK])
        pow2 = sb("pow2", [P, NK])
        two_over = sb("two_over", [P, NK])
        part_scale = sb("part_scale", [P, NK + 1])
        proj_scale = sb("proj_scale", [P, LG + GG])
        proj_tmp = sb("proj_tmp", [P, LG + GG])
        bias_scale = sb("bias_scale", [P, LG + GG + 1])
        act_scale = sb("act_scale", [P, 5])
        h0_shrink = sb("h0_shrink", [P, 1])
        h0_grow = sb("h0_grow", [P, 1])
        bias_raw = sb("bias_raw", [P, (LG + GG + 1) * N])
        bias = sb("bias", [P, (LG + GG + 1) * N])
        h0_sb = sb("h0_sb", [P, NB])
        h0_l = sb("h0_l", [P, NB])
        h0_g = sb("h0_g", [P, NB])

        x_ring = sb("x_ring", [P, XRING, BC])
        x1_ring = sb("x1_ring", [P, XRING, BC])
        y_ring = sb("y_ring", [P, 2, BC])
        x_scaled = sb("x_scaled", [P, BC])
        x1_scaled = sb("x1_scaled", [P, BC])
        x_parts = sb("x_parts", [P, N, 2, BT, B], F16)
        x1_parts = sb("x1_parts", [P, N, 2, BT, B], F16)
        xwl = sb("xwl", [P, 2, LG * N, BT * B])
        xwg = sb("xwg", [P, 2, GG * N, BT * B])
        evac = sb("evac", [P, N, BT * B])

        tl = sb("tl", [P, 2, LG * N, 32, 2])
        pre_l = sb("pre_l", [P, LG * NB])
        gates_l = sb("gates_l", [P, (LG + 1) * NB])
        uv = sb("uv", [P, 2 * NB])
        o_scaled = sb("o_scaled", [P, NB])
        tanh_c = sb("tanh_c", [P, NB])
        h_l = sb("h_l", [P, 2, NB])
        h_l_plain = sb("h_l_plain", [P, 2, NB])
        hl_parts = sb("hl_parts", [P, N, 2 * B], F16)

        tg = sb("tg", [P, 2, GG * N, 32, 2])
        tp = sb("tp", [P, N, 32, 2])
        pre_g = sb("pre_g", [P, GG + 1, NB])
        tanh_r = sb("tanh_r", [P, NB])
        tanh_z = sb("tanh_z", [P, NB])
        cand = sb("cand", [P, NB])
        prop = sb("prop", [P, NB])
        rh = sb("rh", [P, NB])
        zc = sb("zc", [P, NB])
        za = sb("za", [P, NB])
        keep = sb("keep", [P, NB])
        keep_s = sb("keep_s", [P, NB])
        fresh = sb("fresh", [P, NB])
        h_g = sb("h_g", [P, 4, NB])
        h_prop = sb("h_prop", [P, NB])
        hg_parts = sb("hg_parts", [P, N, 4 * B], F16)
        rh_parts = sb("rh_parts", [P, N, 2 * B], F16)
        hp_parts = sb("hp_parts", [P, N, 2 * B], F16)

        ps_l = psum("ps_l", [P, LG * P])
        ps_r = psum("ps_r", [P, 4, P])
        ps_z = psum("ps_z", [P, 4, P])
        ps_c = psum("ps_c", [P, 4, P])
        ps_p = psum("ps_p", [P, 4, P])
        ps_x = psum("ps_x", [P, 2, 2 * N, 2, BT * B])

        small_in = sem("small_in")
        stage_in = [sem(f"stage_in{i}") for i in range(NST)]
        piece_max_s = sem("piece_max_s")
        core_max_s = sem("core_max_s")
        scale_made = sem("scale_made")
        high_part = sem("high_part")
        low_part = sem("low_part")
        setup_chain = sem("setup_chain")
        cleared = sem("cleared")
        consts_ready = sem("consts_ready")
        x_in = sem("x_in")
        y_out = sem("y_out")
        y_ready = sem("y_ready")
        xs_ready = sem("xs_ready")
        x_parts_ready = sem("x_parts_ready")
        x1s_ready = sem("x1s_ready")
        x1_parts_ready = sem("x1_parts_ready")
        x1_done = sem("x1_done")
        h_plain = sem("h_plain")
        proj_l = sem("proj_l")
        proj_g = sem("proj_g")
        evac_sum = sem("evac_sum")
        xwl_ready = sem("xwl_ready")
        xwg_ready = sem("xwg_ready")
        regrown = sem("regrown")
        first_rh = sem("first_rh")
        first_fresh = sem("first_fresh")
        first_keep = sem("first_keep")
        l_mm, l_turned, l_sum, l_gates, l_uv, l_c, l_tc, l_o, l_h1, l_h, l_slot = (
            sem(n) for n in ("l_mm", "l_turned", "l_sum", "l_gates", "l_uv", "l_c", "l_tc", "l_o", "l_h1", "l_h", "l_slot"))
        r_mm, z_mm, c_mm, r_turned, z_turned, c_turned, r_sum, z_sum, c_sum = (
            sem(n) for n in ("r_mm", "z_mm", "c_mm", "r_turned", "z_turned", "c_turned", "r_sum", "z_sum", "c_sum"))
        r_tanh, z_tanh, c_tanh, rh_high, rh_ready, g_slot = (
            sem(n) for n in ("r_tanh", "z_tanh", "c_tanh", "rh_high", "rh_ready", "g_slot"))
        z_affine, keep_high, keep_ready, fresh_high, fresh_ready, hg_ready = (
            sem(n) for n in ("z_affine", "keep_high", "keep_ready", "fresh_high", "fresh_ready", "hg_ready"))
        p_mm, p_turned, p_sum, p_tanh, hp_high, hp_ready = (
            sem(n) for n in ("p_mm", "p_turned", "p_sum", "p_tanh", "hp_high", "hp_ready"))

        block = ctx.enter_context(nc.Block())

        def nb(t):
            return t.rearrange("p (n b) -> p n b", b=B)

        def parts(t, m, k):
            return t[:, :, 0:k * B, :].rearrange("p m (k b) s -> p m b k s", b=B)

        def has_l(k):
            return 0 <= k < NBLK

        def has_g(k):
            return 0 <= k - LAG < NBLK

        MAIN = (LAG + 2, NBLK - 2)

        def phases(eng, body):
            for k in range(0, MAIN[0]):
                body(k, k)
            with eng.Fori(MAIN[0], MAIN[1]) as k:
                body(k, MAIN[0])
            for k in range(MAIN[1], NBLK + LAG):
                body(k, k)

        class Values:

            def __init__(self, eng, base):
                self.eng, self.base, self.kept = eng, base, {}

            def __call__(self, c):
                if isinstance(self.base, int):
                    return self.base + c
                if c not in self.kept:
                    self.kept[c] = self.eng.snap(self.base + c)
                return self.kept[c]

        NX = T * NB // PIECE
        pieces = [("whl", g) for g in range(LG)] + [("x", g) for g in range(NX)]
        pieces += [("wxl", g) for g in range(LG)] + [("whg", g) for g in range(GG + 1)] + [("wxg", g) for g in range(GG)]
        NP = len(pieces)
        group_of = {"whl": lambda g: K_WHL, "x": lambda g: K_X, "wxl": lambda g: K_WXL + g,
                    "whg": lambda g: K_WHG + g, "wxg": lambda g: K_WXG + g}
        last_of = {}
        for i, (what, g) in enumerate(pieces):
            last_of[group_of[what](g)] = i
        first_of = {}
        for i, (what, g) in reversed(list(enumerate(pieces))):
            first_of[group_of[what](g)] = i
        scale_order = [K_H0] + sorted(last_of, key=last_of.get)
        scale_at = {g: n + 1 for n, g in enumerate(scale_order)}
        weight_pieces = [i for i, (what, _) in enumerate(pieces) if what != "x"]
        split_at = {i: n + 1 for n, i in enumerate(weight_pieces)}

        def target(i, w):
            what, g = pieces[i]
            t = {"whl": whl, "whg": whg, "wxl": wxl, "wxg": wxg}[what][w]
            return t[:, g, :, :] if what[1] == "h" else t[:, g, :, :, :].rearrange("p n m c -> p n (m c)")

        def piece_view(i):
            return stage[:, i % NST, :].rearrange("p (n c) -> p n c", n=N)

        def piece_scale(i):
            what, g = pieces[i]
            c = NK if what == "whl" and g == LG - 1 else group_of[what](g)
            return part_scale[:, c:c + 1]

        @block.sync
        def _(sp):
            sp.dma_start(h0_sb[:], h0).then_inc(small_in, 16)
            sp.dma_start(bias_raw[:, 0:LG * N], b_lstm).then_inc(small_in, 16)
            sp.dma_start(bias_raw[:, LG * N:(LG + GG) * N], b_gru).then_inc(small_in, 16)
            sp.dma_start(bias_raw[:, (LG + GG) * N:], b_prop).then_inc(small_in, 16)
            src = {"whl": w_lstm_h, "x": x, "wxl": w_lstm_x, "whg": w_gru_h, "wxg": w_gru_x}
            for i, (what, g) in enumerate(pieces):
                if i >= NST:
                    j = i - NST
                    sp.wait_ge(piece_max_s, j + 2)
                    if j in split_at:
                        sp.wait_ge(low_part, split_at[j])
                sp.dma_start(stage[:, i % NST, :], src[what][:, g * PIECE:(g + 1) * PIECE]).then_inc(stage_in[i % NST], 16)
            for b in range(3):
                if b:
                    sp.wait_ge(x_in, 16 * b)
                sp.dma_start(x_ring[:, b, :], x[:, b * BC:(b + 1) * BC]).then_inc(x_in, 16)

            def body(k, k0):
                if k0 + 3 < NBLK:
                    if k0:
                        sp.wait_ge(x1_done, k * BT)
                    sp.wait_ge(x_in, (k + 3) * 16)
                    sp.dma_start(x_ring[:, bass.ds((k + 3) % XRING, 1), :].rearrange("p r c -> p (r c)"),
                                 x[:, bass.ds((k + 3) * BC, BC)]).then_inc(x_in, 16)
                if k0 - LAG - 1 >= 0:
                    store(k - LAG - 1, k0 - LAG - 1)

            def store(blk, blk0):
                sp.wait_ge(y_ready, (blk + 1) * (BT // 4))
                if blk0 > 0:
                    sp.wait_ge(y_out, blk * 16)
                sp.dma_start(out[:, bass.ds(blk * BC, BC)],
                             y_ring[:, bass.ds(blk % 2, 1), :].rearrange("p r c -> p (r c)")).then_inc(y_out, 16)

            for k in range(0, MAIN[0]):
                body(k, k)
            with sp.Fori(MAIN[0], NBLK - 3) as k:
                body(k, MAIN[0])
            for k in range(NBLK - 3, NBLK + LAG):
                body(k, k)
            store(NBLK - 1, NBLK - 1)
            sp.wait_ge(y_out, NBLK * 16)

        @block.scalar
        def _(act):
            for i in weight_pieces:
                act.wait_ge(stage_in[i % NST], 16 * (i // NST + 1))
                act.wait_ge(scale_made, scale_at[group_of[pieces[i][0]](pieces[i][1])])
                nc.scalar.activation(target(i, 0), piece_view(i), ACT.Identity,
                                     scale=piece_scale(i)).then_inc(high_part, 1)
            act.wait_ge(consts_ready, 1)
            scale_l, scale_r, scale_z, scale_c, scale_p = (act.alloc_register(f"scale_{n}") for n in "lrzcp")
            for n, reg in enumerate((scale_l, scale_r, scale_z, scale_c, scale_p)):
                act.reg_load(reg, act_scale[0:1, n:n + 1].bitcast(I32))

            def body(k, k0):
                L, G = has_l(k0), has_g(k0)
                t, u = Values(act, k * BT), Values(act, (k - LAG) * BT if G else 0)
                for s in range(BT):
                    if G and s % 4 == 0 and (s or has_g(k0 - 1)):
                        act.wait_ge(p_sum, (k - LAG) * (BT // 4) + s // 4)
                        nc.scalar.activation(prop[:], pre_g[:, GG, :], ACT.Tanh, scale=scale_p).then_inc(p_tanh, 1)
                    if L:
                        act.wait_ge(l_sum, t(s + 1))
                        nc.scalar.activation(gates_l[:, 0:LG * NB], pre_l[:], ACT.Tanh, scale=scale_l).then_inc(l_gates, 1)
                    if G:
                        act.wait_ge(r_sum, u(s + 1))
                        nc.scalar.activation(tanh_r[:], pre_g[:, 0, :], ACT.Tanh, scale=scale_r).then_inc(r_tanh, 1)
                    if L:
                        act.wait_ge(l_c, t(s + 1))
                        nc.scalar.activation(tanh_c[:], gates_l[:, LG * NB:], ACT.Tanh, scale=0.5).then_inc(l_tc, 1)
                    if G:
                        act.wait_ge(z_sum, u(s + 1))
                        nc.scalar.activation(tanh_z[:], pre_g[:, 1, :], ACT.Tanh, scale=scale_z).then_inc(z_tanh, 1)
                        act.wait_ge(z_tanh, u(s + 1))
                        nc.scalar.activation(za[:], tanh_z[:], ACT.Copy, scale=-0.5, bias=0.5)
                        nc.scalar.activation(zc[:], tanh_z[:], ACT.Copy, scale=GRU_H / 2, bias=GRU_H / 2).then_inc(z_affine, 1)
                    if L:
                        act.wait_ge(l_h1, t(s + 1))
                        nc.scalar.activation(h_l_plain[:, s % 2, :], h_l[:, s % 2, :], ACT.Copy, scale=1.0 / LSTM_H).then_inc(h_plain, 1)
                    if G:
                        act.wait_ge(c_sum, u(s + 1))
                        nc.scalar.activation(cand[:], pre_g[:, 2, :], ACT.Tanh, scale=scale_c).then_inc(c_tanh, 1)

            phases(act, body)

        @block.gpsimd
        def _(pool):
            def reduce_over_partitions(n):
                pool.wait_ge(piece_max_s, n + 1)
                nc.gpsimd.partition_all_reduce(core_max[:, n:n + 1], piece_max[:, n:n + 1], P, RMAX).then_inc(core_max_s, 1)

            for n in range(NP + 1):
                reduce_over_partitions(n)
            pool.wait_ge(consts_ready, 1)

            def wait(s, v):
                pool.wait_ge(s, v)
                pool.wait_ge(consts_ready, 1)

            def split_x(blk):
                scale = part_scale[:, K_X:K_X + 1].rearrange("p (t n b) -> p t n b", n=1, b=1).broadcast_to([P, BT, N, B])
                if not isinstance(blk, int) or blk > 0:
                    wait(x_parts_ready, blk)
                    wait(proj_l, blk * LG)
                pool.wait_ge(x_in, (blk + 1) * 16)
                src = x_ring[:, bass.ds(blk % XRING, 1), :].rearrange("p r c -> p (r c)")
                nc.gpsimd.tensor_copy(x_scaled[:], src).then_inc(xs_ready, 1)
                wait(xs_ready, 2 * blk + 1)
                v = x_scaled[:].rearrange("p (t n b) -> p t n b", n=N, b=B)
                hi = x_parts[:, :, 0, :, :].rearrange("p n t b -> p t n b")
                lo = x_parts[:, :, 1, :, :].rearrange("p n t b -> p t n b")
                nc.gpsimd.tensor_tensor(hi, v, scale, ALU.mult)
                nc.gpsimd.tensor_tensor(v, v, scale, ALU.mult).then_inc(xs_ready, 1)
                wait(xs_ready, 2 * blk + 2)
                nc.gpsimd.tensor_tensor(lo, v, hi, ALU.subtract).then_inc(x_parts_ready, 1)

            def split_x1(blk):
                scale = part_scale[:, K_X:K_X + 1].rearrange("p (t n b) -> p t n b", n=1, b=1).broadcast_to([P, BT, N, B])
                if not isinstance(blk, int) or blk > 0:
                    wait(x1_parts_ready, blk)
                    wait(proj_g, blk * GG)
                wait(x1_done, (blk + 1) * BT)
                src = x1_ring[:, bass.ds(blk % XRING, 1), :].rearrange("p r c -> p (r c)")
                nc.gpsimd.tensor_copy(x1_scaled[:], src).then_inc(x1s_ready, 1)
                wait(x1s_ready, 2 * blk + 1)
                v = x1_scaled[:].rearrange("p (t n b) -> p t n b", n=N, b=B)
                hi = x1_parts[:, :, 0, :, :].rearrange("p n t b -> p t n b")
                lo = x1_parts[:, :, 1, :, :].rearrange("p n t b -> p t n b")
                nc.gpsimd.tensor_tensor(hi, v, scale, ALU.mult)
                nc.gpsimd.tensor_tensor(v, v, scale, ALU.mult).then_inc(x1s_ready, 1)
                wait(x1s_ready, 2 * blk + 2)
                nc.gpsimd.tensor_tensor(lo, v, hi, ALU.subtract).then_inc(x1_parts_ready, 1)

            def slot_l(blk, s):
                src = xwl[:, bass.ds(blk % 2, 1), :, s * B:(s + 1) * B].rearrange("p r m b -> p (r m) b")
                nc.gpsimd.tensor_copy(tl[:, s % 2, :, 0:B, 1], src).then_inc(l_slot, 1)

            def slot_g(blk, s):
                src = xwg[:, bass.ds(blk % 2, 1), :, s * B:(s + 1) * B].rearrange("p r m b -> p (r m) b")
                nc.gpsimd.tensor_copy(tg[:, s % 2, :, 0:B, 1], src).then_inc(g_slot, 1)

            def lstm_residual(blk, s, done):
                wait(h_plain, done + 1)
                at = (blk % XRING) * BC + s * NB
                dst = x1_ring[:].rearrange("p r c -> p (r c)")[:, bass.ds(at, NB)]
                src = x_ring[:].rearrange("p r c -> p (r c)")[:, bass.ds(at, NB)]
                nc.gpsimd.tensor_tensor(dst, h_l_plain[:, s % 2, :], src, ALU.add).then_inc(x1_done, 1)

            def gru_keep(s, u, prev, first):
                wait(z_affine, u(s + 1))
                hi, lo = hg_parts[:, :, 0:B], hg_parts[:, :, B:2 * B]
                if first:
                    nc.gpsimd.tensor_tensor(keep[:], za[:], prev, ALU.mult).then_inc(first_keep, 1)
                    wait(first_keep, 2 * s + 1)
                    nc.gpsimd.tensor_scalar(keep_s[:], keep[:], h0_shrink[:], None, ALU.mult).then_inc(first_keep, 1)
                    nc.gpsimd.tensor_scalar(hi, nb(keep[:]), h0_shrink[:], None, ALU.mult).then_inc(keep_high, 1)
                    wait(keep_high, u(s + 1))
                    nc.gpsimd.tensor_tensor(lo, nb(keep_s[:]), hi, ALU.subtract).then_inc(keep_ready, 1)
                else:
                    nc.gpsimd.tensor_tensor(keep[:], za[:], prev, ALU.mult)
                    nc.gpsimd.tensor_tensor(hi, nb(za[:]), nb(prev), ALU.mult).then_inc(keep_high, 1)
                    wait(keep_high, u(s + 1))
                    nc.gpsimd.tensor_tensor(lo, nb(keep[:]), hi, ALU.subtract).then_inc(keep_ready, 1)

            split_x(0)
            split_x(1)
            wait(xwl_ready, LG)
            slot_l(0, 0)

            def body(k, k0):
                L, G = has_l(k0), has_g(k0)
                t, u = Values(pool, k * BT), Values(pool, (k - LAG) * BT if G else 0)
                for s in range(BT):
                    first = G and k0 == LAG and s < 4
                    if s and L:
                        lstm_residual(k, s - 1, t(s - 1))
                    if s == 0 and has_l(k0 - 1):
                        lstm_residual(k - 1, BT - 1, k * BT - 1)
                    if s + 1 < BT and L:
                        if s or has_l(k0 - 1):
                            wait(l_sum, t(s))
                        slot_l(k, s + 1)
                    if s + 1 == BT and has_l(k0 + 1):
                        wait(l_sum, t(s))
                        wait(xwl_ready, (k + 2) * LG)
                        slot_l(k + 1, 0)
                    if s + 1 < BT and G:
                        if s or has_g(k0 - 1):
                            wait(c_sum, u(s))
                        slot_g(k - LAG, s + 1)
                    if s + 1 == BT and has_g(k0 + 1):
                        if G:
                            wait(c_sum, u(s))
                        wait(xwg_ready, (k + 2 - LAG) * GG)
                        slot_g(k + 1 - LAG, 0)
                    if G:
                        gru_keep(s, u, h_prop[:] if s % 4 == 0 else h_g[:, s % 4 - 1, :], first)
                    if s == 1 and has_l(k0 - 1):
                        split_x1(k - 1)
                    if s == 9 and has_l(k0 + 2):
                        split_x(k + 2)

            phases(pool, body)

        @block.vector
        def _(dve):
            v = nc.vector
            chained = [0]

            def chain(ins):
                chained[0] += 1
                ins.then_inc(setup_chain, 1)
                dve.wait_ge(setup_chain, chained[0])

            def make_scale(group):
                if group == K_X:
                    chain(v.tensor_scalar(largest[:, K_X:K_X + 1], largest[:, K_X:K_X + 1], 1.0, None, ALU.add))
                m = largest[:, group:group + 1]
                chain(v.tensor_scalar(m, m, 1.0 if group == K_H0 else TINY, None, ALU.max))
                v.tensor_scalar(pow2[:, group:group + 1].bitcast(I32), m.bitcast(I32), EXPONENT, None, ALU.bitwise_and)
                chain(v.tensor_scalar(two_over[:, group:group + 1].bitcast(I32), m.bitcast(I32), EXPONENT, EXPONENT,
                                      ALU.bitwise_and, ALU.bitwise_xor))
                e, t2 = pow2[:, group:group + 1], two_over[:, group:group + 1]
                if group == K_H0:
                    v.tensor_scalar(h0_grow[:], e, 2.0, None, ALU.mult)
                    v.tensor_scalar(h0_shrink[:], t2, 0.25, None, ALU.mult).then_inc(scale_made, 1)
                elif group == K_WHL:
                    v.tensor_scalar(part_scale[:, NK:NK + 1], t2, 2.0 ** 13, None, ALU.mult)
                    v.tensor_scalar(part_scale[:, group:group + 1], t2, 2.0 ** 12, None, ALU.mult).then_inc(scale_made, 1)
                else:
                    v.tensor_scalar(part_scale[:, group:group + 1], t2, 2.0 ** 13, None, ALU.mult).then_inc(scale_made, 1)
                dve.wait_ge(scale_made, scale_at[group])

            for ps in (ps_l[:], ps_r[:], ps_z[:], ps_c[:], ps_p[:]):
                v.memset(ps, 0.0)
            for tt in (tl[:], tg[:], tp[:]):
                v.memset(tt, 0.0)
            v.memset(gates_l[:], 0.0).then_inc(cleared, 1)
            dve.wait_ge(cleared, 1)
            dve.wait_ge(small_in, 64)

            v.tensor_reduce(out=piece_max[:, 0:1], in_=h0_sb[:], axis=AX.X, op=ALU.max,
                            apply_absolute_value=True).then_inc(piece_max_s, 1)

            def piece_largest(i):
                dve.wait_ge(stage_in[i % NST], 16 * (i // NST + 1))
                v.tensor_reduce(out=piece_max[:, i + 1:i + 2], in_=stage[:, i % NST, :], axis=AX.X, op=ALU.max,
                                apply_absolute_value=True).then_inc(piece_max_s, 1)

            def low(i):
                dve.wait_ge(high_part, split_at[i])
                v.scalar_tensor_tensor(out=target(i, 1), in0=piece_view(i), scalar=piece_scale(i), in1=target(i, 0),
                                       op0=ALU.mult, op1=ALU.subtract).then_inc(low_part, 1)

            def group_scale(group, a, b):
                dve.wait_ge(core_max_s, b)
                chain(v.tensor_reduce(out=largest[:, group:group + 1], in_=core_max[:, a:b], axis=AX.X, op=ALU.max))
                make_scale(group)

            group_scale(K_H0, 0, 1)
            pending = []
            for i, (what, g) in enumerate(pieces):
                piece_largest(i)
                for j in pending[:1]:
                    low(j)
                pending = pending[1:]
                group = group_of[what](g)
                if last_of[group] == i:
                    group_scale(group, first_of[group] + 1, i + 2)
                    if what == "whl":
                        for j in range(first_of[group], i + 1):
                            low(j)
                    elif what != "x":
                        pending.append(i)
            for j in pending:
                low(j)

            e_x = pow2[:, K_X:K_X + 1]
            for g in range(LG + GG):
                h = K_WHL if g < LG else K_WHG + g - LG
                xg = K_WXL + g if g < LG else K_WXG + g - LG
                double = 2.0 if g in (LG - 1, LG + GG - 1) else 1.0
                v.tensor_scalar(bias_scale[:, g:g + 1], two_over[:, h:h + 1], double * 2.0 ** 27, None, ALU.mult)
                chain(v.tensor_scalar(proj_tmp[:, g:g + 1], two_over[:, h:h + 1], 0.5 * double, e_x, ALU.mult, ALU.mult))
                v.tensor_scalar(proj_scale[:, g:g + 1], proj_tmp[:, g:g + 1], pow2[:, xg:xg + 1], None, ALU.mult)
            h = K_WHG + GG
            chain(v.tensor_scalar(bias_scale[:, LG + GG:], two_over[:, h:h + 1], 2.0 ** 27, None, ALU.mult))
            for n, (group, f) in enumerate(((K_WHL, -29), (K_WHG, -29), (K_WHG + 1, -29), (K_WHG + 2, -29), (K_WHG + 3, -28))):
                v.tensor_scalar(act_scale[:, n:n + 1], pow2[:, group:group + 1], 2.0 ** f, None, ALU.mult)
            for g in range(LG + GG + 1):
                v.tensor_scalar(bias[:, g * N:(g + 1) * N], bias_raw[:, g * N:(g + 1) * N], bias_scale[:, g:g + 1],
                                None, ALU.mult)
            chain(v.tensor_scalar(h0_l[:], h0_sb[:], LSTM_H, h0_shrink[:], ALU.mult, ALU.mult))
            v.tensor_scalar(h_prop[:], h0_sb[:], GRU_H, None, ALU.mult)
            chain(v.tensor_scalar(h0_g[:], h0_sb[:], GRU_H, h0_shrink[:], ALU.mult, ALU.mult))
            v.tensor_copy(hl_parts[:, :, 0:B], nb(h0_l[:]))
            chain(v.tensor_copy(hp_parts[:, :, 0:B], nb(h0_g[:])))
            v.tensor_tensor(hl_parts[:, :, B:2 * B], nb(h0_l[:]), hl_parts[:, :, 0:B], ALU.subtract)
            chain(v.tensor_tensor(hp_parts[:, :, B:2 * B], nb(h0_g[:]), hp_parts[:, :, 0:B], ALU.subtract))
            for b in range(B):
                last = v.tensor_copy(tp[:, :, b, 1], bias[:, (LG + GG) * N:])
            last.then_inc(consts_ready, 1)

            def evacuate(ps, g_all, dst, ready, mm, mm_value, ev):
                dve.wait_ge(mm, mm_value)
                v.tensor_reduce(out=evac[:], in_=ps.rearrange("p m k c -> p m c k"), axis=AX.X, op=ALU.add).then_inc(evac_sum, 1)
                dve.wait_ge(evac_sum, ev)
                each = bias[:, g_all * N:(g_all + 1) * N].rearrange("p (m o) -> p m o", o=1).broadcast_to([P, N, BT * B])
                v.scalar_tensor_tensor(out=dst, in0=evac[:], scalar=proj_scale[:, g_all:g_all + 1], in1=each,
                                       op0=ALU.mult, op1=ALU.add).then_inc(ready, 1)

            def evac_l(blk, g, ev):
                dst = xwl[:, bass.ds(blk % 2, 1), g * N:(g + 1) * N, :].rearrange("p r m c -> p (r m) c")
                evacuate(ps_x[:, g % 2, 0:N, :, :], g, dst, xwl_ready, proj_l, blk * LG + g + 1, ev)

            def evac_g(blk, g, ev):
                dst = xwg[:, bass.ds(blk % 2, 1), g * N:(g + 1) * N, :].rearrange("p r m c -> p (r m) c")
                evacuate(ps_x[:, g % 2, 0:N, :, :], LG + g, dst, xwg_ready, proj_g, blk * GG + g + 1, ev)

            for g in range(LG):
                if g:
                    dve.wait_ge(xwl_ready, g)
                evac_l(0, g, g + 1)

            regrows = [0]

            def body(k, k0):
                L, G = has_l(k0), has_g(k0)
                t, u = Values(dve, k * BT), Values(dve, (k - LAG) * BT if G else 0)
                ev0 = LG + (LG + GG) * k - GG if k0 > 0 else LG
                if k0 > NBLK - 1:
                    ev0 = LG * NBLK + GG * (k - 1)
                ev = Values(dve, ev0)
                evs = 0

                def turn(ps, dst, mm, val, done):
                    dve.wait_ge(mm, val)
                    v.transpose(dst[:, :, :, 0], ps).then_inc(done, 1)
                    dve.wait_ge(done, val)

                def grow(tt):
                    regrows[0] += 1
                    v.tensor_scalar(tt, tt, h0_grow[:], None, ALU.mult).then_inc(regrown, 1)
                    dve.wait_ge(regrown, regrows[0])

                for s in range(BT):
                    first = G and k0 == LAG and s < 4
                    nparts = 2 if s % 4 == 0 else 4
                    prev = h_prop[:] if s % 4 == 0 else h_g[:, s % 4 - 1, :]
                    tgs = tg[:, s % 2, :, :, :]
                    if G and s % 4 == 0 and (s or has_g(k0 - 1)):
                        pv = Values(dve, (k - LAG) * (BT // 4) + s // 4)
                        turn(ps_p[:, 0, :].rearrange("p (n c) -> p n c", c=32), tp[:], p_mm, pv(0), p_turned)
                        if k0 == LAG and s == 4:
                            grow(tp[:, :, 0:4 * B, 0])
                        v.tensor_reduce(out=nb(pre_g[:, GG, :]), in_=parts(tp[:], N, 4), axis=AX.XY, op=ALU.add).then_inc(p_sum, 1)
                        dve.wait_ge(p_tanh, pv(0))
                        v.tensor_scalar(h_prop[:], prop[:], GRU_H, None, ALU.mult)
                        v.tensor_scalar(hp_parts[:, :, 0:B], nb(prop[:]), GRU_H, None, ALU.mult).then_inc(hp_high, 1)
                        dve.wait_ge(hp_high, pv(0))
                        v.tensor_tensor(hp_parts[:, :, B:2 * B], nb(h_prop[:]), hp_parts[:, :, 0:B], ALU.subtract).then_inc(hp_ready, 1)
                    if L:
                        tls = tl[:, s % 2, :, :, :]
                        turn(ps_l[:].rearrange("p (m c) -> p m c", c=32), tls, l_mm, t(s + 1), l_turned)
                        if k0 == 0 and s == 0:
                            grow(tls[:, :, 0:2 * B, 0])
                        dve.wait_ge(l_slot, t(s + 1))
                        v.tensor_reduce(out=pre_l[:].rearrange("p (m b) -> p m b", b=B), in_=parts(tls, LG * N, 2),
                                        axis=AX.XY, op=ALU.add).then_inc(l_sum, 1)
                    if G:
                        turn(ps_r[:, 0, :].rearrange("p (n c) -> p n c", c=32), tgs[:, 0:N], r_mm, u(s + 1), r_turned)
                        if first:
                            grow(tgs[:, 0:N, 0:nparts * B, 0])
                        dve.wait_ge(g_slot, u(s + 1))
                        v.tensor_reduce(out=nb(pre_g[:, 0, :]), in_=parts(tgs[:, 0:N], N, nparts), axis=AX.XY,
                                        op=ALU.add).then_inc(r_sum, 1)
                    if L:
                        dve.wait_ge(l_gates, t(s + 1))
                        v.scalar_tensor_tensor(out=uv[:], in0=gates_l[:, 0:2 * NB], scalar=1.0, in1=gates_l[:, 3 * NB:5 * NB],
                                               op0=ALU.add, op1=ALU.mult).then_inc(l_uv, 1)
                        dve.wait_ge(l_uv, t(s + 1))
                        v.scalar_tensor_tensor(out=gates_l[:, 4 * NB:5 * NB], in0=uv[:, NB:2 * NB], scalar=0.5, in1=uv[:, 0:NB],
                                               op0=ALU.mult, op1=ALU.add).then_inc(l_c, 1)
                    if G:
                        dve.wait_ge(r_tanh, u(s + 1))
                        hi, lo = rh_parts[:, :, 0:B], rh_parts[:, :, B:2 * B]
                        if first:
                            v.scalar_tensor_tensor(out=rh[:], in0=tanh_r[:], scalar=1.0, in1=prev, op0=ALU.add,
                                                   op1=ALU.mult).then_inc(first_rh, 1)
                            dve.wait_ge(first_rh, s + 1)
                            v.tensor_scalar(hi, nb(rh[:]), h0_shrink[:], None, ALU.mult).then_inc(rh_high, 1)
                            dve.wait_ge(rh_high, u(s + 1))
                            v.scalar_tensor_tensor(out=lo, in0=nb(rh[:]), scalar=h0_shrink[:], in1=hi, op0=ALU.mult,
                                                   op1=ALU.subtract).then_inc(rh_ready, 1)
                        else:
                            v.scalar_tensor_tensor(out=rh[:], in0=tanh_r[:], scalar=1.0, in1=prev, op0=ALU.add, op1=ALU.mult)
                            v.scalar_tensor_tensor(out=hi, in0=nb(tanh_r[:]), scalar=1.0, in1=nb(prev), op0=ALU.add,
                                                   op1=ALU.mult).then_inc(rh_high, 1)
                    if L:
                        v.tensor_scalar(o_scaled[:], gates_l[:, 2 * NB:3 * NB], LSTM_H / 2, LSTM_H / 2, ALU.mult,
                                        ALU.add).then_inc(l_o, 1)
                    if G and not first:
                        dve.wait_ge(rh_high, u(s + 1))
                        v.tensor_tensor(lo, nb(rh[:]), hi, ALU.subtract).then_inc(rh_ready, 1)
                    if G:
                        turn(ps_z[:, 0, :].rearrange("p (n c) -> p n c", c=32), tgs[:, N:2 * N], z_mm, u(s + 1), z_turned)
                        if first:
                            grow(tgs[:, N:2 * N, 0:nparts * B, 0])
                        v.tensor_reduce(out=nb(pre_g[:, 1, :]), in_=parts(tgs[:, N:2 * N], N, nparts), axis=AX.XY,
                                        op=ALU.add).then_inc(z_sum, 1)
                    if L:
                        dve.wait_ge(l_o, t(s + 1))
                        dve.wait_ge(l_tc, t(s + 1))
                        v.tensor_tensor(h_l[:, s % 2, :], o_scaled[:], tanh_c[:], ALU.mult)
                        v.tensor_tensor(hl_parts[:, :, 0:B], nb(o_scaled[:]), nb(tanh_c[:]), ALU.mult).then_inc(l_h1, 1)
                        dve.wait_ge(l_h1, t(s + 1))
                        v.tensor_tensor(hl_parts[:, :, B:2 * B], nb(h_l[:, s % 2, :]), hl_parts[:, :, 0:B],
                                        ALU.subtract).then_inc(l_h, 1)
                    if G:
                        turn(ps_c[:, 0, :].rearrange("p (n c) -> p n c", c=32), tgs[:, 2 * N:3 * N], c_mm, u(s + 1), c_turned)
                        if first:
                            grow(tgs[:, 2 * N:3 * N, 0:2 * B, 0])
                        v.tensor_reduce(out=nb(pre_g[:, 2, :]), in_=parts(tgs[:, 2 * N:3 * N], N, 2), axis=AX.XY,
                                        op=ALU.add).then_inc(c_sum, 1)
                        dve.wait_ge(z_affine, u(s + 1))
                        dve.wait_ge(c_tanh, u(s + 1))
                        hi, lo = hg_parts[:, :, 2 * B:3 * B], hg_parts[:, :, 3 * B:4 * B]
                        if first:
                            v.tensor_tensor(fresh[:], zc[:], cand[:], ALU.mult).then_inc(first_fresh, 1)
                            dve.wait_ge(first_fresh, s + 1)
                            v.tensor_scalar(hi, nb(fresh[:]), h0_shrink[:], None, ALU.mult).then_inc(fresh_high, 1)
                            dve.wait_ge(fresh_high, u(s + 1))
                            v.scalar_tensor_tensor(out=lo, in0=nb(fresh[:]), scalar=h0_shrink[:], in1=hi, op0=ALU.mult,
                                                   op1=ALU.subtract).then_inc(fresh_ready, 1)
                        else:
                            v.tensor_tensor(fresh[:], zc[:], cand[:], ALU.mult)
                            v.tensor_tensor(hi, nb(zc[:]), nb(cand[:]), ALU.mult).then_inc(fresh_high, 1)
                            dve.wait_ge(fresh_high, u(s + 1))
                            v.tensor_tensor(lo, nb(fresh[:]), hi, ALU.subtract).then_inc(fresh_ready, 1)
                        dve.wait_ge(keep_high, u(s + 1))
                        v.tensor_tensor(h_g[:, s % 4, :], keep[:], fresh[:], ALU.add).then_inc(hg_ready, 1)
                    if s % 2 and s < 2 * LG and has_l(k0 + 1):
                        evs += 1
                        evac_l(k + 1, s // 2, ev(evs))
                    if s % 2 and 2 * LG <= s < 2 * (LG + GG) and has_l(k0 - 1):
                        evs += 1
                        evac_g(k - 1, s // 2 - LG, ev(evs))
                    if G and s % 4 == 3:
                        dve.wait_ge(hg_ready, u(s + 1))
                        if s == 3 and k0 - LAG >= 1:
                            dve.wait_ge(y_out, (k - LAG - 1) * 16)
                        blk = k - LAG
                        flat = x1_ring[:].rearrange("p r c -> p (r c)")
                        yflat = y_ring[:].rearrange("p r c -> p (r c)")
                        v.scalar_tensor_tensor(out=yflat[:, bass.ds((blk % 2) * BC + (s - 3) * NB, 4 * NB)],
                                               in0=h_g[:].rearrange("p t c -> p (t c)"), scalar=1.0 / GRU_H,
                                               in1=flat[:, bass.ds((blk % XRING) * BC + (s - 3) * NB, 4 * NB)],
                                               op0=ALU.mult, op1=ALU.add).then_inc(y_ready, 1)

            phases(dve, body)

        @block.tensor
        def _(pe):
            mm = nc.tensor.matmul

            def lstm_rounds(lo, hi):
                for r in range(lo, hi):
                    n, w = r // 2, r % 2
                    for j in range(4):
                        last = mm(ps_l[32 * j:32 * j + 2 * B, :].rearrange("p (g c) -> p g c", g=LG), hl_parts[:, n, :],
                                  whl[w][:, :, n, P * j:P * (j + 1)], start=(r == 0), stop=(r == 2 * N - 1))
                return last

            def gru_rounds(ps, state, gate):
                rows = state.shape[2]
                for r in range(2 * N):
                    n, w = r // 2, r % 2
                    for j in range(4):
                        last = mm(ps[32 * j:32 * j + rows, 0, :], state[:, n, :], whg[w][:, gate, n, P * j:P * (j + 1)],
                                  start=(r == 0), stop=(r == 2 * N - 1))
                return last

            def project(wx, xp, g, tiles):
                for m in tiles:
                    for r in range(2 * N):
                        n, w = r // 2, r % 2
                        last = mm(ps_x[:, g % 2, m, :, :].rearrange("p k c -> p (k c)"), wx[w][:, g, n, m, :],
                                  xp[:, n, :, :, :].rearrange("p k t b -> p (k t b)"), start=(r == 0), stop=(r == 2 * N - 1))
                return last

            pe.wait_ge(low_part, len(weight_pieces))
            pe.wait_ge(cleared, 1)
            pe.wait_ge(x_parts_ready, 1)
            for g in range(LG):
                if g >= 2:
                    pe.wait_ge(xwl_ready, g - 1)
                project(wxl, x_parts, g, range(N)).then_inc(proj_l, 1)
            pe.wait_ge(consts_ready, 1)

            def body(k, k0):
                L, G = has_l(k0), has_g(k0)
                t, u = Values(pe, k * BT), Values(pe, (k - LAG) * BT if G else 0)
                for s in range(BT):
                    p_due = G and s % 4 == 0 and (s or has_g(k0 - 1))
                    cut = 5 if p_due else 2 * N
                    if L:
                        if s or k0:
                            pe.wait_ge(l_h, t(s))
                        last = lstm_rounds(0, cut)
                    if p_due:
                        pe.wait_ge(keep_ready, u(s))
                        pe.wait_ge(fresh_ready, u(s))
                        gru_rounds(ps_p, hg_parts, GG).then_inc(p_mm, 1)
                        if L:
                            last = lstm_rounds(cut, 2 * N)
                    if L:
                        last.then_inc(l_mm, 1)
                    if G:
                        if p_due:
                            pe.wait_ge(hp_ready, (k - LAG) * (BT // 4) + s // 4)
                        elif s:
                            pe.wait_ge(keep_ready, u(s))
                            pe.wait_ge(fresh_ready, u(s))
                        state = hp_parts if s % 4 == 0 else hg_parts
                        gru_rounds(ps_r, state, 0).then_inc(r_mm, 1)
                        gru_rounds(ps_z, state, 1).then_inc(z_mm, 1)
                    half, g = s % 2, s // 2
                    if s < 2 * LG and has_l(k0 + 1):
                        if s == 0:
                            pe.wait_ge(x_parts_ready, k + 2)
                            if k0 == 0:
                                pe.wait_ge(xwl_ready, LG)
                        last = project(wxl, x_parts, g, range(2 * half, 2 * half + 2))
                        if half:
                            last.then_inc(proj_l, 1)
                    if 2 * LG <= s < 2 * (LG + GG) and has_l(k0 - 1):
                        if s == 2 * LG:
                            pe.wait_ge(x1_parts_ready, k)
                        last = project(wxg, x1_parts, g - LG, range(2 * half, 2 * half + 2))
                        if half:
                            last.then_inc(proj_g, 1)
                    if G:
                        pe.wait_ge(rh_ready, u(s + 1))
                        gru_rounds(ps_c, rh_parts, 2).then_inc(c_mm, 1)

            phases(pe, body)


def kernel(x, cond_1024, L0_cond_Wx, L0_cond_Wh, L0_cond_b, L1_cond_Wz, L1_cond_bz, L1_cond_Wr, L1_cond_br,
           L1_cond_Wh, L1_cond_bh, L1_cond_Wp, L1_cond_bp):
    import numpy as np
    from concourse import bacc
    from concourse.bass_utils import run_bass_kernel_spmd

    T = x.shape[1]

    def rows(w):
        return w.reshape(4, N, 32, -1).transpose(0, 2, 1, 3).reshape(P, N, -1)

    def columns(w):
        return w.reshape(w.shape[:-1] + (-1, 4, N, 32)).swapaxes(-3, -2).reshape(w.shape[:-1] + (-1, N, P))

    def recurrent(w):
        return np.ascontiguousarray(rows(w).reshape(P, N, -1, D).transpose(0, 2, 1, 3)).reshape(P, -1)

    def projecting(w):
        return np.ascontiguousarray(columns(rows(w)).transpose(0, 2, 1, 3, 4)).reshape(P, -1)

    def bias(b):
        return np.ascontiguousarray(columns(b[None])[0].transpose(2, 0, 1)).reshape(P, -1)

    x, h0 = np.asarray(x), np.asarray(cond_1024)
    wr, wz, wh = (np.asarray(w) for w in (L1_cond_Wr, L1_cond_Wz, L1_cond_Wh))
    gru_in = np.concatenate([wr[:D], wz[:D], wh[:D]], axis=1)
    gru_state = np.concatenate([wr[D:], wz[D:], wh[D:], np.asarray(L1_cond_Wp)], axis=1)
    gru_bias = np.concatenate([np.asarray(b) for b in (L1_cond_br, L1_cond_bz, L1_cond_bh)])
    arrays = {
        "x": np.ascontiguousarray(x.reshape(B, T, 4, N, 32).transpose(2, 4, 1, 3, 0)).reshape(P, -1),
        "h0": np.ascontiguousarray(h0.reshape(B, 4, N, 32).transpose(1, 3, 2, 0)).reshape(P, -1),
        "w_lstm_x": projecting(np.asarray(L0_cond_Wx)),
        "w_lstm_h": recurrent(np.asarray(L0_cond_Wh)),
        "b_lstm": bias(np.asarray(L0_cond_b)),
        "w_gru_x": projecting(gru_in),
        "w_gru_h": recurrent(gru_state),
        "b_gru": bias(gru_bias),
        "b_prop": bias(np.asarray(L1_cond_bp)),
    }
    nc = bacc.Bacc("TRN2", target_bir_lowering=False, num_devices=1)
    aps = {n: nc.dram_tensor(f"in_{n}", a.shape, F32, kind="ExternalInput").ap() for n, a in arrays.items()}
    out = nc.dram_tensor("out", (P, T * NB), F32, kind="ExternalOutput").ap()
    cond_resid_kernel(nc, *aps.values(), out)
    r = run_bass_kernel_spmd(nc, [{f"in_{n}": a for n, a in arrays.items()}], core_ids=[0])
    y = r.results[0]["out"].reshape(4, 32, T, N, B)
    return np.ascontiguousarray(y.transpose(4, 2, 0, 3, 1)).reshape(B, T, D)
```

```python
from contextlib import ExitStack

import concourse.bass as bass
from concourse import mybir

P = 128
F32 = mybir.dt.float32
F16 = mybir.dt.float16
I32 = mybir.dt.int32
ACT = mybir.ActivationFunctionType
ALU = mybir.AluOpType
AX = mybir.AxisListType
RMAX = bass.bass_isa.ReduceOp.max

B = 2
D = 512
N = D // P
NB = N * B
LG = 4
GG = 3
BT = 16
BC = BT * NB
PIECE = N * D
XRING = 4
LAG = 2
LSTM_ROUNDS_BEFORE_P = 5

EXPONENT = 0x7F800000
TINY = 2.0 ** -40
LSTM_H = 2.0 ** 15
GRU_H = 2.0 ** 14

K_WHL, K_WHG, K_WXL, K_WXG, K_X, K_H0 = 0, 1, 5, 9, 12, 13
NK = 14


def cond_resid_kernel(nc, x, h0, w_lstm_x, w_lstm_h, b_lstm, w_gru_x, w_gru_h, b_gru, b_prop, out):
    T = x.shape[1] // NB
    NBLK = T // BT
    with ExitStack() as ctx:
        def sb(name, shape, dt=F32):
            return ctx.enter_context(nc.sbuf_tensor(name, shape, dt))

        def psum(name, shape):
            return ctx.enter_context(nc.psum_tensor(name, shape, F32))

        def sem(name):
            return ctx.enter_context(nc.semaphore(name))

        whl = [sb(f"whl{w}", [P, LG, N, D], F16) for w in range(2)]
        whg = [sb(f"whg{w}", [P, GG + 1, N, D], F16) for w in range(2)]
        wxl = [sb(f"wxl{w}", [P, LG, N, N, P], F16) for w in range(2)]
        wxg = [sb(f"wxg{w}", [P, GG, N, N, P], F16) for w in range(2)]
        NST = 4
        stage = sb("stage", [P, NST, PIECE])

        piece_max = sb("piece_max", [P, 24])
        core_max = sb("core_max", [P, 24])
        largest = sb("largest", [P, NK])
        pow2 = sb("pow2", [P, NK])
        two_over = sb("two_over", [P, NK])
        part_scale = sb("part_scale", [P, NK + 1])
        proj_scale = sb("proj_scale", [P, LG + GG])
        proj_tmp = sb("proj_tmp", [P, LG + GG])
        bias_scale = sb("bias_scale", [P, LG + GG + 1])
        act_scale = sb("act_scale", [P, 5])
        h0_shrink = sb("h0_shrink", [P, 1])
        h0_grow = sb("h0_grow", [P, 1])
        bias_raw = sb("bias_raw", [P, (LG + GG + 1) * N])
        bias = sb("bias", [P, (LG + GG + 1) * N])
        h0_sb = sb("h0_sb", [P, NB])
        h0_l = sb("h0_l", [P, NB])
        h0_g = sb("h0_g", [P, NB])

        x_ring = sb("x_ring", [P, XRING, BC])
        x1_ring = sb("x1_ring", [P, XRING, BC])
        y_ring = sb("y_ring", [P, 2, BC])
        x_scaled = sb("x_scaled", [P, BC])
        x1_scaled = sb("x1_scaled", [P, BC])
        x_parts = sb("x_parts", [P, N, 2, BT, B], F16)
        x1_parts = sb("x1_parts", [P, N, 2, BT, B], F16)
        xwl = sb("xwl", [P, 2, LG * N, BT * B])
        xwg = sb("xwg", [P, 2, GG * N, BT * B])
        evac = sb("evac", [P, N, BT * B])

        tl = sb("tl", [P, 2, LG * N, 32, 2])
        pre_l = sb("pre_l", [P, LG * NB])
        gates_l = sb("gates_l", [P, (LG + 1) * NB])
        uv = sb("uv", [P, 2 * NB])
        o_scaled = sb("o_scaled", [P, NB])
        tanh_c = sb("tanh_c", [P, NB])
        h_l = sb("h_l", [P, 2, NB])
        h_l_plain = sb("h_l_plain", [P, 2, NB])
        hl_parts = sb("hl_parts", [P, N, 2 * B], F16)

        tg = sb("tg", [P, 2, (GG - 1) * N, 32, 2])
        pre_g = sb("pre_g", [P, GG + 1, NB])
        tanh_r = sb("tanh_r", [P, NB])
        tanh_z = sb("tanh_z", [P, NB])
        cand = sb("cand", [P, NB])
        prop = sb("prop", [P, NB])
        rh = sb("rh", [P, NB])
        zc = sb("zc", [P, NB])
        za = sb("za", [P, NB])
        keep = sb("keep", [P, NB])
        keep_s = sb("keep_s", [P, NB])
        fresh = sb("fresh", [P, NB])
        h_g = sb("h_g", [P, 4, NB])
        h_prop = sb("h_prop", [P, NB])
        hg_parts = sb("hg_parts", [P, N, 4 * B], F16)
        rh_parts = sb("rh_parts", [P, N, 2 * B], F16)
        hp_parts = sb("hp_parts", [P, N, 2 * B], F16)

        ps_l = psum("ps_l", [P, LG * P])
        ps_r = psum("ps_r", [P, N, D // N // B, B])
        ps_p = psum("ps_p", [P, N, D // N // B, B])
        ps_z = psum("ps_z", [P, 4, P])
        ps_c = psum("ps_c", [P, 4, P])
        ps_x = psum("ps_x", [P, 2, 2 * N, 2, BT * B])

        small_in = sem("small_in")
        stage_in = [sem(f"stage_in{i}") for i in range(NST)]
        piece_max_s = sem("piece_max_s")
        core_max_s = sem("core_max_s")
        scale_made = sem("scale_made")
        high_part = sem("high_part")
        low_part = sem("low_part")
        setup_chain = sem("setup_chain")
        cleared = sem("cleared")
        consts_ready = sem("consts_ready")
        x_in = sem("x_in")
        y_out = sem("y_out")
        y_ready = sem("y_ready")
        xs_ready = sem("xs_ready")
        x_parts_ready = sem("x_parts_ready")
        x1s_ready = sem("x1s_ready")
        x1_parts_ready = sem("x1_parts_ready")
        x1_done = sem("x1_done")
        h_plain = sem("h_plain")
        proj_l = sem("proj_l")
        proj_g = sem("proj_g")
        evac_sum = sem("evac_sum")
        xwl_ready = sem("xwl_ready")
        xwg_ready = sem("xwg_ready")
        regrown = sem("regrown")
        first_rh = sem("first_rh")
        first_fresh = sem("first_fresh")
        first_keep = sem("first_keep")
        l_mm, l_turned, l_sum, l_gates, l_uv, l_c, l_tc, l_o, l_h1, l_h, l_slot = (
            sem(n) for n in ("l_mm", "l_turned", "l_sum", "l_gates", "l_uv", "l_c", "l_tc", "l_o", "l_h1", "l_h", "l_slot"))
        r_slot, r_mm, z_mm, c_mm, z_turned, c_turned, r_sum, z_sum, c_sum = (
            sem(n) for n in ("r_slot", "r_mm", "z_mm", "c_mm", "z_turned", "c_turned", "r_sum", "z_sum", "c_sum"))
        r_tanh, z_tanh, c_tanh, rh_high, rh_ready, g_slot = (
            sem(n) for n in ("r_tanh", "z_tanh", "c_tanh", "rh_high", "rh_ready", "g_slot"))
        z_affine, keep_high, keep_ready, fresh_high, fresh_ready, hg_ready = (
            sem(n) for n in ("z_affine", "keep_high", "keep_ready", "fresh_high", "fresh_ready", "hg_ready"))
        p_mm, p_sum, p_tanh, hp_high, hp_ready = (
            sem(n) for n in ("p_mm", "p_sum", "p_tanh", "hp_high", "hp_ready"))

        block = ctx.enter_context(nc.Block())

        def nb(t):
            return t.rearrange("p (n b) -> p n b", b=B)

        def parts(t, m, k):
            return t[:, :, 0:k * B, :].rearrange("p m (k b) s -> p m b k s", b=B)

        TILES = (LG + GG) * N
        tiles_before, tiles_behind, done = [], [], 0
        for s in range(BT):
            before, behind = ((3, 1), (0, 1), (0, 1), (0, 1))[s % 4]
            for lot, n in ((tiles_before, before), (tiles_behind, behind)):
                n = min(n, TILES - done)
                lot.append(range(done, done + n))
                done += n
        gates_done = [[m // N for m in [*tiles_before[s], *tiles_behind[s]] if m % N == N - 1] for s in range(BT)]

        def has_l(k):
            return 0 <= k < NBLK

        def has_g(k):
            return 0 <= k - LAG < NBLK

        def evacuated(k, k0):
            if k0 > NBLK - 1:
                return LG * NBLK + GG * (k - 1)
            return LG + (LG + GG) * k - GG if k0 > 0 else LG

        MAIN = (LAG + 2, NBLK - 2)

        def phases(eng, body):
            for k in range(0, MAIN[0]):
                body(k, k)
            with eng.Fori(MAIN[0], MAIN[1]) as k:
                body(k, MAIN[0])
            for k in range(MAIN[1], NBLK + LAG):
                body(k, k)

        def r_first(s):
            return not tiles_before[s]

        class Values:

            def __init__(self, eng, base):
                self.eng, self.base, self.kept = eng, base, {}

            def __call__(self, c):
                if isinstance(self.base, int):
                    return self.base + c
                if c not in self.kept:
                    self.kept[c] = self.eng.snap(self.base + c)
                return self.kept[c]

        NX = T * NB // PIECE
        pieces = [("whl", g) for g in range(LG)] + [("x", g) for g in range(NX)]
        pieces += [("wxl", g) for g in range(LG)] + [("whg", g) for g in range(GG + 1)] + [("wxg", g) for g in range(GG)]
        NP = len(pieces)
        group_of = {"whl": lambda g: K_WHL, "x": lambda g: K_X, "wxl": lambda g: K_WXL + g,
                    "whg": lambda g: K_WHG + g, "wxg": lambda g: K_WXG + g}
        last_of = {}
        for i, (what, g) in enumerate(pieces):
            last_of[group_of[what](g)] = i
        first_of = {}
        for i, (what, g) in reversed(list(enumerate(pieces))):
            first_of[group_of[what](g)] = i
        scale_order = [K_H0] + sorted(last_of, key=last_of.get)
        scale_at = {g: n + 1 for n, g in enumerate(scale_order)}
        weight_pieces = [i for i, (what, _) in enumerate(pieces) if what != "x"]
        split_at = {i: n + 1 for n, i in enumerate(weight_pieces)}

        def target(i, w):
            what, g = pieces[i]
            t = {"whl": whl, "whg": whg, "wxl": wxl, "wxg": wxg}[what][w]
            return t[:, g, :, :] if what[1] == "h" else t[:, g, :, :, :].rearrange("p n m c -> p n (m c)")

        def piece_view(i):
            return stage[:, i % NST, :].rearrange("p (n c) -> p n c", n=N)

        def piece_scale(i):
            what, g = pieces[i]
            c = NK if what == "whl" and g == LG - 1 else group_of[what](g)
            return part_scale[:, c:c + 1]

        @block.sync
        def _(sp):
            sp.dma_start(h0_sb[:], h0).then_inc(small_in, 16)
            sp.dma_start(bias_raw[:, 0:LG * N], b_lstm).then_inc(small_in, 16)
            sp.dma_start(bias_raw[:, LG * N:(LG + GG) * N], b_gru).then_inc(small_in, 16)
            sp.dma_start(bias_raw[:, (LG + GG) * N:], b_prop).then_inc(small_in, 16)
            src = {"whl": w_lstm_h, "x": x, "wxl": w_lstm_x, "whg": w_gru_h, "wxg": w_gru_x}
            for i, (what, g) in enumerate(pieces):
                if i >= NST:
                    j = i - NST
                    sp.wait_ge(piece_max_s, j + 2)
                    if j in split_at:
                        sp.wait_ge(low_part, split_at[j])
                sp.dma_start(stage[:, i % NST, :], src[what][:, g * PIECE:(g + 1) * PIECE]).then_inc(stage_in[i % NST], 16)
            for b in range(3):
                if b:
                    sp.wait_ge(x_in, 16 * b)
                sp.dma_start(x_ring[:, b, :], x[:, b * BC:(b + 1) * BC]).then_inc(x_in, 16)

            def body(k, k0):
                if k0 + 3 < NBLK:
                    if k0:
                        sp.wait_ge(x1_done, k * BT)
                    sp.wait_ge(x_in, (k + 3) * 16)
                    sp.dma_start(x_ring[:, bass.ds((k + 3) % XRING, 1), :].rearrange("p r c -> p (r c)"),
                                 x[:, bass.ds((k + 3) * BC, BC)]).then_inc(x_in, 16)
                if k0 - LAG - 1 >= 0:
                    store(k - LAG - 1, k0 - LAG - 1)

            def store(blk, blk0):
                sp.wait_ge(y_ready, (blk + 1) * (BT // 4))
                if blk0 > 0:
                    sp.wait_ge(y_out, blk * 16)
                sp.dma_start(out[:, bass.ds(blk * BC, BC)],
                             y_ring[:, bass.ds(blk % 2, 1), :].rearrange("p r c -> p (r c)")).then_inc(y_out, 16)

            for k in range(0, MAIN[0]):
                body(k, k)
            with sp.Fori(MAIN[0], NBLK - 3) as k:
                body(k, MAIN[0])
            for k in range(NBLK - 3, NBLK + LAG):
                body(k, k)
            store(NBLK - 1, NBLK - 1)
            sp.wait_ge(y_out, NBLK * 16)

        @block.scalar
        def _(act):
            for i in weight_pieces:
                act.wait_ge(stage_in[i % NST], 16 * (i // NST + 1))
                act.wait_ge(scale_made, scale_at[group_of[pieces[i][0]](pieces[i][1])])
                nc.scalar.activation(target(i, 0), piece_view(i), ACT.Identity,
                                     scale=piece_scale(i)).then_inc(high_part, 1)
            act.wait_ge(consts_ready, 1)
            scale_l, scale_r, scale_z, scale_c, scale_p = (act.alloc_register(f"scale_{n}") for n in "lrzcp")
            for n, reg in enumerate((scale_l, scale_r, scale_z, scale_c, scale_p)):
                act.reg_load(reg, act_scale[0:1, n:n + 1].bitcast(I32))

            def slot_r(blk, s):
                src = xwg[:, bass.ds(blk % 2, 1), 0:N, s * B:(s + 1) * B].rearrange("p r m b -> p (r m) b")
                nc.scalar.copy(ps_r[:, :, 4, :], src).then_inc(r_slot, 1)

            def tanh_of_r(step):
                act.wait_ge(r_sum, step)
                nc.scalar.activation(tanh_r[:], pre_g[:, 0, :], ACT.Tanh, scale=scale_r).then_inc(r_tanh, 1)

            def body(k, k0):
                L, G = has_l(k0), has_g(k0)
                t, u = Values(act, k * BT), Values(act, (k - LAG) * BT if G else 0)
                for s in range(BT):
                    if G and s % 4 == 0 and (s or has_g(k0 - 1)):
                        act.wait_ge(p_sum, (k - LAG) * (BT // 4) + s // 4)
                        nc.scalar.activation(prop[:], pre_g[:, GG, :], ACT.Tanh, scale=scale_p).then_inc(p_tanh, 1)
                    if G and r_first(s):
                        tanh_of_r(u(s + 1))
                    if L:
                        act.wait_ge(l_sum, t(s + 1))
                        nc.scalar.activation(gates_l[:, 0:LG * NB], pre_l[:], ACT.Tanh, scale=scale_l).then_inc(l_gates, 1)
                    if G and not r_first(s):
                        tanh_of_r(u(s + 1))
                    if L:
                        act.wait_ge(l_c, t(s + 1))
                        nc.scalar.activation(tanh_c[:], gates_l[:, LG * NB:], ACT.Tanh, scale=0.5).then_inc(l_tc, 1)
                    if G:
                        act.wait_ge(z_sum, u(s + 1))
                        nc.scalar.activation(tanh_z[:], pre_g[:, 1, :], ACT.Tanh, scale=scale_z).then_inc(z_tanh, 1)
                        act.wait_ge(z_tanh, u(s + 1))
                        nc.scalar.activation(za[:], tanh_z[:], ACT.Copy, scale=-0.5, bias=0.5)
                        nc.scalar.activation(zc[:], tanh_z[:], ACT.Copy, scale=GRU_H / 2, bias=GRU_H / 2).then_inc(z_affine, 1)
                    if L:
                        act.wait_ge(l_h1, t(s + 1))
                        nc.scalar.activation(h_l_plain[:, s % 2, :], h_l[:, s % 2, :], ACT.Copy, scale=1.0 / LSTM_H).then_inc(h_plain, 1)
                    if G:
                        act.wait_ge(c_sum, u(s + 1))
                        nc.scalar.activation(cand[:], pre_g[:, 2, :], ACT.Tanh, scale=scale_c).then_inc(c_tanh, 1)
                    if G and s + 1 < BT:
                        slot_r(k - LAG, s + 1)
                    if s + 1 == BT and has_g(k0 + 1):
                        act.wait_ge(xwg_ready, (k + 2 - LAG) * GG)
                        slot_r(k + 1 - LAG, 0)

            phases(act, body)

        @block.gpsimd
        def _(pool):
            def reduce_over_partitions(n):
                pool.wait_ge(piece_max_s, n + 1)
                nc.gpsimd.partition_all_reduce(core_max[:, n:n + 1], piece_max[:, n:n + 1], P, RMAX).then_inc(core_max_s, 1)

            for n in range(NP + 1):
                reduce_over_partitions(n)
            pool.wait_ge(consts_ready, 1)

            def wait(s, v):
                pool.wait_ge(s, v)
                pool.wait_ge(consts_ready, 1)

            def split_x(blk):
                scale = part_scale[:, K_X:K_X + 1].rearrange("p (t n b) -> p t n b", n=1, b=1).broadcast_to([P, BT, N, B])
                if not isinstance(blk, int) or blk > 0:
                    wait(x_parts_ready, blk)
                    wait(proj_l, blk * LG)
                pool.wait_ge(x_in, (blk + 1) * 16)
                src = x_ring[:, bass.ds(blk % XRING, 1), :].rearrange("p r c -> p (r c)")
                nc.gpsimd.tensor_copy(x_scaled[:], src).then_inc(xs_ready, 1)
                wait(xs_ready, 2 * blk + 1)
                v = x_scaled[:].rearrange("p (t n b) -> p t n b", n=N, b=B)
                hi = x_parts[:, :, 0, :, :].rearrange("p n t b -> p t n b")
                lo = x_parts[:, :, 1, :, :].rearrange("p n t b -> p t n b")
                nc.gpsimd.tensor_tensor(hi, v, scale, ALU.mult)
                nc.gpsimd.tensor_tensor(v, v, scale, ALU.mult).then_inc(xs_ready, 1)
                wait(xs_ready, 2 * blk + 2)
                nc.gpsimd.tensor_tensor(lo, v, hi, ALU.subtract).then_inc(x_parts_ready, 1)

            def split_x1(blk):
                scale = part_scale[:, K_X:K_X + 1].rearrange("p (t n b) -> p t n b", n=1, b=1).broadcast_to([P, BT, N, B])
                if not isinstance(blk, int) or blk > 0:
                    wait(x1_parts_ready, blk)
                    wait(proj_g, blk * GG)
                wait(x1_done, (blk + 1) * BT)
                src = x1_ring[:, bass.ds(blk % XRING, 1), :].rearrange("p r c -> p (r c)")
                nc.gpsimd.tensor_copy(x1_scaled[:], src).then_inc(x1s_ready, 1)
                wait(x1s_ready, 2 * blk + 1)
                v = x1_scaled[:].rearrange("p (t n b) -> p t n b", n=N, b=B)
                hi = x1_parts[:, :, 0, :, :].rearrange("p n t b -> p t n b")
                lo = x1_parts[:, :, 1, :, :].rearrange("p n t b -> p t n b")
                nc.gpsimd.tensor_tensor(hi, v, scale, ALU.mult)
                nc.gpsimd.tensor_tensor(v, v, scale, ALU.mult).then_inc(x1s_ready, 1)
                wait(x1s_ready, 2 * blk + 2)
                nc.gpsimd.tensor_tensor(lo, v, hi, ALU.subtract).then_inc(x1_parts_ready, 1)

            def slot_l(blk, s):
                src = xwl[:, bass.ds(blk % 2, 1), :, s * B:(s + 1) * B].rearrange("p r m b -> p (r m) b")
                nc.gpsimd.tensor_copy(tl[:, s % 2, :, 0:B, 1], src).then_inc(l_slot, 1)

            def slot_g(blk, s):
                src = xwg[:, bass.ds(blk % 2, 1), N:GG * N, s * B:(s + 1) * B].rearrange("p r m b -> p (r m) b")
                nc.gpsimd.tensor_copy(tg[:, s % 2, :, 0:B, 1], src).then_inc(g_slot, 1)

            def lstm_residual(blk, s, done):
                wait(h_plain, done + 1)
                at = (blk % XRING) * BC + s * NB
                dst = x1_ring[:].rearrange("p r c -> p (r c)")[:, bass.ds(at, NB)]
                src = x_ring[:].rearrange("p r c -> p (r c)")[:, bass.ds(at, NB)]
                nc.gpsimd.tensor_tensor(dst, h_l_plain[:, s % 2, :], src, ALU.add).then_inc(x1_done, 1)

            def gru_keep(s, u, prev, first):
                wait(z_affine, u(s + 1))
                hi, lo = hg_parts[:, :, 0:B], hg_parts[:, :, B:2 * B]
                if first:
                    nc.gpsimd.tensor_tensor(keep[:], za[:], prev, ALU.mult).then_inc(first_keep, 1)
                    wait(first_keep, 2 * s + 1)
                    nc.gpsimd.tensor_scalar(keep_s[:], keep[:], h0_shrink[:], None, ALU.mult).then_inc(first_keep, 1)
                    nc.gpsimd.tensor_scalar(hi, nb(keep[:]), h0_shrink[:], None, ALU.mult).then_inc(keep_high, 1)
                    wait(keep_high, u(s + 1))
                    nc.gpsimd.tensor_tensor(lo, nb(keep_s[:]), hi, ALU.subtract).then_inc(keep_ready, 1)
                else:
                    nc.gpsimd.tensor_tensor(keep[:], za[:], prev, ALU.mult)
                    nc.gpsimd.tensor_tensor(hi, nb(za[:]), nb(prev), ALU.mult).then_inc(keep_high, 1)
                    wait(keep_high, u(s + 1))
                    nc.gpsimd.tensor_tensor(lo, nb(keep[:]), hi, ALU.subtract).then_inc(keep_ready, 1)

            split_x(0)
            split_x(1)
            wait(xwl_ready, LG)
            slot_l(0, 0)

            def body(k, k0):
                L, G = has_l(k0), has_g(k0)
                t, u = Values(pool, k * BT), Values(pool, (k - LAG) * BT if G else 0)
                for s in range(BT):
                    first = G and k0 == LAG and s < 4
                    if s and L:
                        lstm_residual(k, s - 1, t(s - 1))
                    if s == 0 and has_l(k0 - 1):
                        lstm_residual(k - 1, BT - 1, k * BT - 1)
                    if s + 1 < BT and L:
                        if s or has_l(k0 - 1):
                            wait(l_sum, t(s))
                        slot_l(k, s + 1)
                    if s + 1 == BT and has_l(k0 + 1):
                        wait(l_sum, t(s))
                        wait(xwl_ready, (k + 2) * LG)
                        slot_l(k + 1, 0)
                    if s + 1 < BT and G:
                        if s or has_g(k0 - 1):
                            wait(c_sum, u(s))
                        slot_g(k - LAG, s + 1)
                    if G:
                        gru_keep(s, u, h_prop[:] if s % 4 == 0 else h_g[:, s % 4 - 1, :], first)
                    if s + 1 == BT and has_g(k0 + 1):
                        if G:
                            wait(c_sum, u(s))
                        wait(xwg_ready, (k + 2 - LAG) * GG)
                        slot_g(k + 1 - LAG, 0)
                    if s == 1 and has_l(k0 - 1):
                        split_x1(k - 1)
                    if s == 9 and has_l(k0 + 2):
                        split_x(k + 2)

            phases(pool, body)

        @block.vector
        def _(dve):
            v = nc.vector
            chained = [0]

            def chain(ins):
                chained[0] += 1
                ins.then_inc(setup_chain, 1)
                dve.wait_ge(setup_chain, chained[0])

            def make_scale(group):
                if group == K_X:
                    chain(v.tensor_scalar(largest[:, K_X:K_X + 1], largest[:, K_X:K_X + 1], 1.0, None, ALU.add))
                m = largest[:, group:group + 1]
                chain(v.tensor_scalar(m, m, 1.0 if group == K_H0 else TINY, None, ALU.max))
                v.tensor_scalar(pow2[:, group:group + 1].bitcast(I32), m.bitcast(I32), EXPONENT, None, ALU.bitwise_and)
                chain(v.tensor_scalar(two_over[:, group:group + 1].bitcast(I32), m.bitcast(I32), EXPONENT, EXPONENT,
                                      ALU.bitwise_and, ALU.bitwise_xor))
                e, t2 = pow2[:, group:group + 1], two_over[:, group:group + 1]
                if group == K_H0:
                    v.tensor_scalar(h0_grow[:], e, 2.0, None, ALU.mult)
                    v.tensor_scalar(h0_shrink[:], t2, 0.25, None, ALU.mult).then_inc(scale_made, 1)
                elif group == K_WHL:
                    v.tensor_scalar(part_scale[:, NK:NK + 1], t2, 2.0 ** 13, None, ALU.mult)
                    v.tensor_scalar(part_scale[:, group:group + 1], t2, 2.0 ** 12, None, ALU.mult).then_inc(scale_made, 1)
                else:
                    v.tensor_scalar(part_scale[:, group:group + 1], t2, 2.0 ** 13, None, ALU.mult).then_inc(scale_made, 1)
                dve.wait_ge(scale_made, scale_at[group])

            for ps in (ps_l[:], ps_z[:], ps_c[:]):
                v.memset(ps, 0.0)
            for tt in (tl[:], tg[:]):
                v.memset(tt, 0.0)
            v.memset(gates_l[:], 0.0).then_inc(cleared, 1)
            dve.wait_ge(cleared, 1)
            dve.wait_ge(small_in, 64)

            v.tensor_reduce(out=piece_max[:, 0:1], in_=h0_sb[:], axis=AX.X, op=ALU.max,
                            apply_absolute_value=True).then_inc(piece_max_s, 1)

            def piece_largest(i):
                dve.wait_ge(stage_in[i % NST], 16 * (i // NST + 1))
                v.tensor_reduce(out=piece_max[:, i + 1:i + 2], in_=stage[:, i % NST, :], axis=AX.X, op=ALU.max,
                                apply_absolute_value=True).then_inc(piece_max_s, 1)

            def low(i):
                dve.wait_ge(high_part, split_at[i])
                v.scalar_tensor_tensor(out=target(i, 1), in0=piece_view(i), scalar=piece_scale(i), in1=target(i, 0),
                                       op0=ALU.mult, op1=ALU.subtract).then_inc(low_part, 1)

            def group_scale(group, a, b):
                dve.wait_ge(core_max_s, b)
                chain(v.tensor_reduce(out=largest[:, group:group + 1], in_=core_max[:, a:b], axis=AX.X, op=ALU.max))
                make_scale(group)

            group_scale(K_H0, 0, 1)
            pending = []
            for i, (what, g) in enumerate(pieces):
                piece_largest(i)
                for j in pending[:1]:
                    low(j)
                pending = pending[1:]
                group = group_of[what](g)
                if last_of[group] == i:
                    group_scale(group, first_of[group] + 1, i + 2)
                    if what == "whl":
                        for j in range(first_of[group], i + 1):
                            low(j)
                    elif what != "x":
                        pending.append(i)
            for j in pending:
                low(j)

            e_x = pow2[:, K_X:K_X + 1]
            for g in range(LG + GG):
                h = K_WHL if g < LG else K_WHG + g - LG
                xg = K_WXL + g if g < LG else K_WXG + g - LG
                double = 2.0 if g in (LG - 1, LG + GG - 1) else 1.0
                v.tensor_scalar(bias_scale[:, g:g + 1], two_over[:, h:h + 1], double * 2.0 ** 27, None, ALU.mult)
                chain(v.tensor_scalar(proj_tmp[:, g:g + 1], two_over[:, h:h + 1], 0.5 * double, e_x, ALU.mult, ALU.mult))
                v.tensor_scalar(proj_scale[:, g:g + 1], proj_tmp[:, g:g + 1], pow2[:, xg:xg + 1], None, ALU.mult)
            h = K_WHG + GG
            chain(v.tensor_scalar(bias_scale[:, LG + GG:], two_over[:, h:h + 1], 2.0 ** 27, None, ALU.mult))
            for n, (group, f) in enumerate(((K_WHL, -29), (K_WHG, -29), (K_WHG + 1, -29), (K_WHG + 2, -29), (K_WHG + 3, -28))):
                v.tensor_scalar(act_scale[:, n:n + 1], pow2[:, group:group + 1], 2.0 ** f, None, ALU.mult)
            for g in range(LG + GG + 1):
                v.tensor_scalar(bias[:, g * N:(g + 1) * N], bias_raw[:, g * N:(g + 1) * N], bias_scale[:, g:g + 1],
                                None, ALU.mult)
            chain(v.tensor_scalar(h0_l[:], h0_sb[:], LSTM_H, h0_shrink[:], ALU.mult, ALU.mult))
            v.tensor_scalar(h_prop[:], h0_sb[:], GRU_H, None, ALU.mult)
            chain(v.tensor_scalar(h0_g[:], h0_sb[:], GRU_H, h0_shrink[:], ALU.mult, ALU.mult))
            v.tensor_copy(hl_parts[:, :, 0:B], nb(h0_l[:]))
            chain(v.tensor_copy(hp_parts[:, :, 0:B], nb(h0_g[:])))
            v.tensor_tensor(hl_parts[:, :, B:2 * B], nb(h0_l[:]), hl_parts[:, :, 0:B], ALU.subtract)
            chain(v.tensor_tensor(hp_parts[:, :, B:2 * B], nb(h0_g[:]), hp_parts[:, :, 0:B], ALU.subtract))
            for b in range(B):
                last = v.tensor_copy(ps_p[:, :, 4, b], bias[:, (LG + GG) * N:])
            last.then_inc(consts_ready, 1)

            def evacuate(ps, g_all, dst, ready, mm, mm_value, ev):
                dve.wait_ge(mm, mm_value)
                v.tensor_reduce(out=evac[:], in_=ps.rearrange("p m k c -> p m c k"), axis=AX.X, op=ALU.add).then_inc(evac_sum, 1)
                dve.wait_ge(evac_sum, ev)
                each = bias[:, g_all * N:(g_all + 1) * N].rearrange("p (m o) -> p m o", o=1).broadcast_to([P, N, BT * B])
                v.scalar_tensor_tensor(out=dst, in0=evac[:], scalar=proj_scale[:, g_all:g_all + 1], in1=each,
                                       op0=ALU.mult, op1=ALU.add).then_inc(ready, 1)

            def evac_l(blk, g, ev):
                dst = xwl[:, bass.ds(blk % 2, 1), g * N:(g + 1) * N, :].rearrange("p r m c -> p (r m) c")
                evacuate(ps_x[:, g % 2, 0:N, :, :], g, dst, xwl_ready, proj_l, blk * LG + g + 1, ev)

            def evac_g(blk, g, ev):
                dst = xwg[:, bass.ds(blk % 2, 1), g * N:(g + 1) * N, :].rearrange("p r m c -> p (r m) c")
                evacuate(ps_x[:, g % 2, 0:N, :, :], LG + g, dst, xwg_ready, proj_g, blk * GG + g + 1, ev)

            for g in range(LG):
                if g:
                    dve.wait_ge(xwl_ready, g)
                evac_l(0, g, g + 1)

            regrows = [0]

            def body(k, k0):
                L, G = has_l(k0), has_g(k0)
                t, u = Values(dve, k * BT), Values(dve, (k - LAG) * BT if G else 0)
                ev = Values(dve, evacuated(k, k0))
                evs = 0

                def turn(ps, dst, mm, val, done):
                    dve.wait_ge(mm, val)
                    v.transpose(dst[:, :, :, 0], ps).then_inc(done, 1)
                    dve.wait_ge(done, val)

                def beside(ps, k):
                    return ps[:, :, 4 - k:5, :].rearrange("p n k b -> p n b k")

                def lstm_c():
                    v.scalar_tensor_tensor(out=gates_l[:, 4 * NB:5 * NB], in0=uv[:, NB:2 * NB], scalar=0.5, in1=uv[:, 0:NB],
                                           op0=ALU.mult, op1=ALU.add).then_inc(l_c, 1)

                def grow(tt):
                    regrows[0] += 1
                    v.tensor_scalar(tt, tt, h0_grow[:], None, ALU.mult).then_inc(regrown, 1)
                    dve.wait_ge(regrown, regrows[0])

                def r_total(s, step, first, nparts):
                    dve.wait_ge(r_mm, step)
                    if first:
                        grow(ps_r[:, :, 4 - nparts:4, :])
                    v.tensor_reduce(out=nb(pre_g[:, 0, :]), in_=beside(ps_r, nparts), axis=AX.X, op=ALU.add).then_inc(r_sum, 1)

                def r_times_h(s, step, prev, first):
                    dve.wait_ge(r_tanh, step)
                    hi, lo = rh_parts[:, :, 0:B], rh_parts[:, :, B:2 * B]
                    if first:
                        v.scalar_tensor_tensor(out=rh[:], in0=tanh_r[:], scalar=1.0, in1=prev, op0=ALU.add,
                                               op1=ALU.mult).then_inc(first_rh, 1)
                        dve.wait_ge(first_rh, s + 1)
                        v.tensor_scalar(hi, nb(rh[:]), h0_shrink[:], None, ALU.mult).then_inc(rh_high, 1)
                        dve.wait_ge(rh_high, step)
                        v.scalar_tensor_tensor(out=lo, in0=nb(rh[:]), scalar=h0_shrink[:], in1=hi, op0=ALU.mult,
                                               op1=ALU.subtract).then_inc(rh_ready, 1)
                    else:
                        v.scalar_tensor_tensor(out=rh[:], in0=tanh_r[:], scalar=1.0, in1=prev, op0=ALU.add, op1=ALU.mult)
                        v.scalar_tensor_tensor(out=hi, in0=nb(tanh_r[:]), scalar=1.0, in1=nb(prev), op0=ALU.add,
                                               op1=ALU.mult).then_inc(rh_high, 1)

                def rh_low(step):
                    dve.wait_ge(rh_high, step)
                    v.tensor_tensor(rh_parts[:, :, B:2 * B], nb(rh[:]), rh_parts[:, :, 0:B], ALU.subtract).then_inc(rh_ready, 1)

                for s in range(BT):
                    first = G and k0 == LAG and s < 4
                    nparts = 2 if s % 4 == 0 else 4
                    prev = h_prop[:] if s % 4 == 0 else h_g[:, s % 4 - 1, :]
                    tgs = tg[:, s % 2, :, :, :]
                    if G and s % 4 == 0 and (s or has_g(k0 - 1)):
                        pv = Values(dve, (k - LAG) * (BT // 4) + s // 4)
                        dve.wait_ge(p_mm, pv(0))
                        if k0 == LAG and s == 4:
                            grow(ps_p[:, :, 0:4, :])
                        v.tensor_reduce(out=nb(pre_g[:, GG, :]), in_=beside(ps_p, 4), axis=AX.X, op=ALU.add).then_inc(p_sum, 1)
                        dve.wait_ge(p_tanh, pv(0))
                        v.tensor_scalar(h_prop[:], prop[:], GRU_H, None, ALU.mult)
                        v.tensor_scalar(hp_parts[:, :, 0:B], nb(prop[:]), GRU_H, None, ALU.mult).then_inc(hp_high, 1)
                        dve.wait_ge(hp_high, pv(0))
                        v.tensor_tensor(hp_parts[:, :, B:2 * B], nb(h_prop[:]), hp_parts[:, :, 0:B], ALU.subtract).then_inc(hp_ready, 1)
                    if L:
                        tls = tl[:, s % 2, :, :, :]
                        turn(ps_l[:].rearrange("p (m c) -> p m c", c=32), tls, l_mm, t(s + 1), l_turned)
                        if k0 == 0 and s == 0:
                            grow(tls[:, :, 0:2 * B, 0])
                    if G and r_first(s):
                        r_total(s, u(s + 1), first, nparts)
                    if L:
                        dve.wait_ge(l_slot, t(s + 1))
                        v.tensor_reduce(out=pre_l[:].rearrange("p (m b) -> p m b", b=B), in_=parts(tls, LG * N, 2),
                                        axis=AX.XY, op=ALU.add).then_inc(l_sum, 1)
                    if G and not r_first(s):
                        r_total(s, u(s + 1), first, nparts)
                    if G and r_first(s):
                        r_times_h(s, u(s + 1), prev, first)
                    if L:
                        dve.wait_ge(l_gates, t(s + 1))
                        v.scalar_tensor_tensor(out=uv[:], in0=gates_l[:, 0:2 * NB], scalar=1.0, in1=gates_l[:, 3 * NB:5 * NB],
                                               op0=ALU.add, op1=ALU.mult).then_inc(l_uv, 1)
                    if G and not first and r_first(s):
                        rh_low(u(s + 1))
                    if L and not G:
                        dve.wait_ge(l_uv, t(s + 1))
                        lstm_c()
                    if G and not r_first(s):
                        r_times_h(s, u(s + 1), prev, first)
                    if L and G:
                        dve.wait_ge(l_uv, t(s + 1))
                        lstm_c()
                    if L:
                        v.tensor_scalar(o_scaled[:], gates_l[:, 2 * NB:3 * NB], LSTM_H / 2, LSTM_H / 2, ALU.mult,
                                        ALU.add).then_inc(l_o, 1)
                    if G and not first and not r_first(s):
                        rh_low(u(s + 1))
                    if G:
                        dve.wait_ge(z_mm, u(s + 1))
                        v.transpose(tgs[:, 0:N, :, 0], ps_z[:, 0, :].rearrange("p (n c) -> p n c", c=32)).then_inc(z_turned, 1)
                    if L:
                        dve.wait_ge(l_o, t(s + 1))
                        dve.wait_ge(l_tc, t(s + 1))
                        v.tensor_tensor(h_l[:, s % 2, :], o_scaled[:], tanh_c[:], ALU.mult)
                        v.tensor_tensor(hl_parts[:, :, 0:B], nb(o_scaled[:]), nb(tanh_c[:]), ALU.mult).then_inc(l_h1, 1)
                    if G:
                        dve.wait_ge(z_turned, u(s + 1))
                        if first:
                            grow(tgs[:, 0:N, 0:nparts * B, 0])
                        dve.wait_ge(g_slot, u(s + 1))
                        v.tensor_reduce(out=nb(pre_g[:, 1, :]), in_=parts(tgs[:, 0:N], N, nparts), axis=AX.XY,
                                        op=ALU.add).then_inc(z_sum, 1)
                    if L:
                        dve.wait_ge(l_h1, t(s + 1))
                        v.tensor_tensor(hl_parts[:, :, B:2 * B], nb(h_l[:, s % 2, :]), hl_parts[:, :, 0:B],
                                        ALU.subtract).then_inc(l_h, 1)
                    if G:
                        turn(ps_c[:, 0, :].rearrange("p (n c) -> p n c", c=32), tgs[:, N:2 * N], c_mm, u(s + 1), c_turned)
                        if first:
                            grow(tgs[:, N:2 * N, 0:2 * B, 0])
                        v.tensor_reduce(out=nb(pre_g[:, 2, :]), in_=parts(tgs[:, N:2 * N], N, 2), axis=AX.XY,
                                        op=ALU.add).then_inc(c_sum, 1)
                        dve.wait_ge(z_affine, u(s + 1))
                        dve.wait_ge(c_tanh, u(s + 1))
                        hi, lo = hg_parts[:, :, 2 * B:3 * B], hg_parts[:, :, 3 * B:4 * B]
                        if first:
                            v.tensor_tensor(fresh[:], zc[:], cand[:], ALU.mult).then_inc(first_fresh, 1)
                            dve.wait_ge(first_fresh, s + 1)
                            v.tensor_scalar(hi, nb(fresh[:]), h0_shrink[:], None, ALU.mult).then_inc(fresh_high, 1)
                            dve.wait_ge(fresh_high, u(s + 1))
                            v.scalar_tensor_tensor(out=lo, in0=nb(fresh[:]), scalar=h0_shrink[:], in1=hi, op0=ALU.mult,
                                                   op1=ALU.subtract).then_inc(fresh_ready, 1)
                        else:
                            v.tensor_tensor(fresh[:], zc[:], cand[:], ALU.mult)
                            v.tensor_tensor(hi, nb(zc[:]), nb(cand[:]), ALU.mult).then_inc(fresh_high, 1)
                            dve.wait_ge(fresh_high, u(s + 1))
                            v.tensor_tensor(lo, nb(fresh[:]), hi, ALU.subtract).then_inc(fresh_ready, 1)
                        dve.wait_ge(keep_high, u(s + 1))
                        v.tensor_tensor(h_g[:, s % 4, :], keep[:], fresh[:], ALU.add).then_inc(hg_ready, 1)
                    for g in gates_done[s]:
                        if g < LG and has_l(k0 + 1):
                            evs += 1
                            evac_l(k + 1, g, ev(evs))
                        if g >= LG and has_l(k0 - 1):
                            evs += 1
                            evac_g(k - 1, g - LG, ev(evs))
                    if G and s % 4 == 3:
                        dve.wait_ge(hg_ready, u(s + 1))
                        if s == 3 and k0 - LAG >= 1:
                            dve.wait_ge(y_out, (k - LAG - 1) * 16)
                        blk = k - LAG
                        flat = x1_ring[:].rearrange("p r c -> p (r c)")
                        yflat = y_ring[:].rearrange("p r c -> p (r c)")
                        v.scalar_tensor_tensor(out=yflat[:, bass.ds((blk % 2) * BC + (s - 3) * NB, 4 * NB)],
                                               in0=h_g[:].rearrange("p t c -> p (t c)"), scalar=1.0 / GRU_H,
                                               in1=flat[:, bass.ds((blk % XRING) * BC + (s - 3) * NB, 4 * NB)],
                                               op0=ALU.mult, op1=ALU.add).then_inc(y_ready, 1)

            phases(dve, body)

        @block.tensor
        def _(pe):
            mm = nc.tensor.matmul

            def lstm_rounds(lo, hi):
                for r in range(lo, hi):
                    n, w = r // 2, r % 2
                    for j in range(4):
                        last = mm(ps_l[32 * j:32 * j + 2 * B, :].rearrange("p (g c) -> p g c", g=LG), hl_parts[:, n, :],
                                  whl[w][:, :, n, P * j:P * (j + 1)], start=(r == 0), stop=(r == 2 * N - 1))
                return last

            def gru_rounds(ps, state, gate):
                rows = state.shape[2]
                for r in range(2 * N):
                    n, w = r // 2, r % 2
                    for j in range(4):
                        last = mm(ps[32 * j:32 * j + rows, 0, :], state[:, n, :], whg[w][:, gate, n, P * j:P * (j + 1)],
                                  start=(r == 0), stop=(r == 2 * N - 1))
                return last

            def gru_tiles(ps, state, gate):
                k = state.shape[2] // B
                for m in range(N):
                    for r in range(2 * N):
                        n, w = r // 2, r % 2
                        last = mm(ps[:, m, 4 - k:4, :].rearrange("p k b -> p (k b)"), whg[w][:, gate, n, m * P:(m + 1) * P],
                                  state[:, n, :], start=(r == 0), stop=(r == 2 * N - 1))
                return last

            def project(wx, xp, g, tiles):
                for m in tiles:
                    for r in range(2 * N):
                        n, w = r // 2, r % 2
                        last = mm(ps_x[:, g % 2, m, :, :].rearrange("p k c -> p (k c)"), wx[w][:, g, n, m, :],
                                  xp[:, n, :, :, :].rearrange("p k t b -> p (k t b)"), start=(r == 0), stop=(r == 2 * N - 1))
                return last

            pe.wait_ge(low_part, len(weight_pieces))
            pe.wait_ge(cleared, 1)
            pe.wait_ge(x_parts_ready, 1)
            for g in range(LG):
                if g >= 2:
                    pe.wait_ge(xwl_ready, g - 1)
                project(wxl, x_parts, g, range(N)).then_inc(proj_l, 1)
            pe.wait_ge(consts_ready, 1)

            def project_tiles(k, k0, tiles, ev):
                for m in tiles:
                    g = m // N
                    gates_before = g if has_l(k0 + 1) else g - LG
                    if m % N == 0 and gates_before >= 0 and has_l(k0 + 1 if g < LG else k0 - 1):
                        pe.wait_ge(evac_sum, ev(max(gates_before - 1, 0)))
                    if g < LG and has_l(k0 + 1):
                        if m == 0:
                            pe.wait_ge(x_parts_ready, k + 2)
                        last = project(wxl, x_parts, g, range(m % N, m % N + 1))
                        if m % N == N - 1:
                            last.then_inc(proj_l, 1)
                    if g >= LG and has_l(k0 - 1):
                        if m == LG * N:
                            pe.wait_ge(x1_parts_ready, k)
                        last = project(wxg, x1_parts, g - LG, range(m % N, m % N + 1))
                        if m % N == N - 1:
                            last.then_inc(proj_g, 1)

            def body(k, k0):
                L, G = has_l(k0), has_g(k0)
                t, u = Values(pe, k * BT), Values(pe, (k - LAG) * BT if G else 0)
                ev = Values(pe, evacuated(k, k0))
                for s in range(BT):
                    p_due = G and s % 4 == 0 and (s or has_g(k0 - 1))
                    cut = LSTM_ROUNDS_BEFORE_P if p_due else 2 * N
                    if L:
                        if s or k0:
                            pe.wait_ge(l_h, t(s))
                        last = lstm_rounds(0, cut)
                    if p_due:
                        pe.wait_ge(keep_ready, u(s))
                        pe.wait_ge(fresh_ready, u(s))
                        gru_tiles(ps_p, hg_parts, GG).then_inc(p_mm, 1)
                        if L:
                            last = lstm_rounds(cut, 2 * N)
                    if L:
                        last.then_inc(l_mm, 1)
                    project_tiles(k, k0, tiles_before[s], ev)
                    if G:
                        if p_due:
                            pe.wait_ge(hp_ready, (k - LAG) * (BT // 4) + s // 4)
                        elif s:
                            pe.wait_ge(keep_ready, u(s))
                            pe.wait_ge(fresh_ready, u(s))
                        state = hp_parts if s % 4 == 0 else hg_parts
                        pe.wait_ge(r_slot, u(s + 1))
                        gru_tiles(ps_r, state, 0).then_inc(r_mm, 1)
                        gru_rounds(ps_z, state, 1).then_inc(z_mm, 1)
                    project_tiles(k, k0, tiles_behind[s], ev)
                    if G:
                        pe.wait_ge(rh_ready, u(s + 1))
                        gru_rounds(ps_c, rh_parts, 2).then_inc(c_mm, 1)

            phases(pe, body)


def kernel(x, cond_1024, L0_cond_Wx, L0_cond_Wh, L0_cond_b, L1_cond_Wz, L1_cond_bz, L1_cond_Wr, L1_cond_br,
           L1_cond_Wh, L1_cond_bh, L1_cond_Wp, L1_cond_bp):
    import numpy as np
    from concourse import bacc
    from concourse.bass_utils import run_bass_kernel_spmd

    T = x.shape[1]

    def rows(w):
        return w.reshape(4, N, 32, -1).transpose(0, 2, 1, 3).reshape(P, N, -1)

    def columns(w):
        return w.reshape(w.shape[:-1] + (-1, 4, N, 32)).swapaxes(-3, -2).reshape(w.shape[:-1] + (-1, N, P))

    def recurrent(w):
        return np.ascontiguousarray(rows(w).reshape(P, N, -1, D).transpose(0, 2, 1, 3)).reshape(P, -1)

    def projecting(w):
        return np.ascontiguousarray(columns(rows(w)).transpose(0, 2, 1, 3, 4)).reshape(P, -1)

    def bias(b):
        return np.ascontiguousarray(columns(b[None])[0].transpose(2, 0, 1)).reshape(P, -1)

    x, h0 = np.asarray(x), np.asarray(cond_1024)
    wr, wz, wh = (np.asarray(w) for w in (L1_cond_Wr, L1_cond_Wz, L1_cond_Wh))
    gru_in = np.concatenate([wr[:D], wz[:D], wh[:D]], axis=1)
    wr_state, wp = (columns(w).reshape(D, D) for w in (wr[D:], np.asarray(L1_cond_Wp)))
    gru_state = np.concatenate([wr_state, wz[D:], wh[D:], wp], axis=1)
    gru_bias = np.concatenate([np.asarray(b) for b in (L1_cond_br, L1_cond_bz, L1_cond_bh)])
    arrays = {
        "x": np.ascontiguousarray(x.reshape(B, T, 4, N, 32).transpose(2, 4, 1, 3, 0)).reshape(P, -1),
        "h0": np.ascontiguousarray(h0.reshape(B, 4, N, 32).transpose(1, 3, 2, 0)).reshape(P, -1),
        "w_lstm_x": projecting(np.asarray(L0_cond_Wx)),
        "w_lstm_h": recurrent(np.asarray(L0_cond_Wh)),
        "b_lstm": bias(np.asarray(L0_cond_b)),
        "w_gru_x": projecting(gru_in),
        "w_gru_h": recurrent(gru_state),
        "b_gru": bias(gru_bias),
        "b_prop": bias(np.asarray(L1_cond_bp)),
    }
    nc = bacc.Bacc("TRN2", target_bir_lowering=False, num_devices=1)
    aps = {n: nc.dram_tensor(f"in_{n}", a.shape, F32, kind="ExternalInput").ap() for n, a in arrays.items()}
    out = nc.dram_tensor("out", (P, T * NB), F32, kind="ExternalOutput").ap()
    cond_resid_kernel(nc, *aps.values(), out)
    r = run_bass_kernel_spmd(nc, [{f"in_{n}": a for n, a in arrays.items()}], core_ids=[0])
    y = r.results[0]["out"].reshape(4, 32, T, N, B)
    return np.ascontiguousarray(y.transpose(4, 2, 0, 3, 1)).reshape(B, T, D)
```
